# Optimizing a Trainium2 kernel written in Bass

```python
import numpy as np
import jax
import jax.numpy as jnp

def _softmax(x, axis=-1):
    return jax.nn.softmax(x, axis=axis)

def _gelu(x):
    return jax.nn.gelu(x, approximate=True)

def _silu(x):
    return jax.nn.silu(x)

def _sigmoid(x):
    return jax.nn.sigmoid(x)

def _layernorm(x, axis=-1, eps=1e-05):
    m = jnp.mean(x, axis=axis, keepdims=True)
    v = jnp.var(x, axis=axis, keepdims=True)
    return (x - m) / jnp.sqrt(v + eps)

def _scatter_add(tgt, idx, src, axis=0):
    return tgt.at[idx].add(src)

def _segment_sum(src, seg, n):
    return jax.ops.segment_sum(src, seg, n)
kernel_name = 'mk_adaln_d1_jaxref_r4_3610c8'

def setup_inputs(seed: int=0):
    np.random.seed(seed)
    _w = jnp.asarray

    def _L0_attn_setup():
        import jax, jax.numpy as jnp
        import numpy as np
        DIM = 256
        HEADS = 16
        HEAD_DIM = DIM // HEADS
        BLOCK = 32
        FEAT = 128
        EPS = 1e-08
        key = jax.random.key(seed)
        ks = jax.random.split(key, 5)
        b, n = (4, 1024)
        x = jax.random.normal(ks[0], (b, n, DIM), dtype=jnp.float32)
        Wqkv = jax.random.normal(ks[1], (DIM, 3 * DIM), dtype=jnp.float32) / np.sqrt(DIM)
        proj = jax.random.normal(ks[2], (HEADS, HEAD_DIM, FEAT), dtype=jnp.float32) / np.sqrt(HEAD_DIM)
        Wout = jax.random.normal(ks[3], (DIM, DIM), dtype=jnp.float32) / np.sqrt(DIM)
        bout = jnp.zeros((DIM,), dtype=jnp.float32)
        return {'x': x, 'Wqkv': Wqkv, 'proj': proj, 'Wout': Wout, 'bout': bout}
    _L0_attn_in = _L0_attn_setup()

    def _L0_ffn_setup():
        import jax, jax.numpy as jnp
        import numpy as np
        D_MODEL, FF_DIM = (256, 512)
        N_SHARED, N_ROUTED, TOP_K = (1, 8, 2)
        BATCH, SEQ = (2, 512)
        key = jax.random.key(seed)
        ks = jax.random.split(key, 8)
        init = lambda k, shape: jax.random.normal(k, shape, jnp.float32) * 0.02
        x = jax.random.normal(ks[0], (BATCH, SEQ, D_MODEL), jnp.float32)
        Wg = init(ks[1], (D_MODEL, N_ROUTED))
        Ws1 = init(ks[2], (D_MODEL, FF_DIM))
        Ws3 = init(ks[3], (D_MODEL, FF_DIM))
        Ws2 = init(ks[4], (FF_DIM, D_MODEL))
        We1 = init(ks[5], (N_ROUTED, D_MODEL, FF_DIM))
        We3 = init(ks[6], (N_ROUTED, D_MODEL, FF_DIM))
        We2 = init(ks[7], (N_ROUTED, FF_DIM, D_MODEL))
        return {'x': x, 'Wg': Wg, 'Ws1': Ws1, 'Ws3': Ws3, 'Ws2': Ws2, 'We1': We1, 'We3': We3, 'We2': We2}
    _L0_ffn_in = _L0_ffn_setup()
    _L0_c = _w((lambda *s: np.random.randn(*s).astype(np.float32) * 0.05)(8, 256))
    _L0_wmod = _w((lambda *s: np.random.randn(*s).astype(np.float32) * 0.05)(256, 6 * 256) * 256 ** (-0.5))
    _d = {'L0_attn_x': _L0_attn_in['x'], 'L0_attn_Wqkv': _L0_attn_in['Wqkv'], 'L0_attn_proj': _L0_attn_in['proj'], 'L0_attn_Wout': _L0_attn_in['Wout'], 'L0_attn_bout': _L0_attn_in['bout'], 'L0_ffn_Wg': _L0_ffn_in['Wg'], 'L0_ffn_Ws1': _L0_ffn_in['Ws1'], 'L0_ffn_Ws3': _L0_ffn_in['Ws3'], 'L0_ffn_Ws2': _L0_ffn_in['Ws2'], 'L0_ffn_We1': _L0_ffn_in['We1'], 'L0_ffn_We3': _L0_ffn_in['We3'], 'L0_ffn_We2': _L0_ffn_in['We2'], 'L0_c': _L0_c, 'L0_wmod': _L0_wmod}
    _x0 = _d['L0_attn_x']
    _d['L0_attn_x'] = jax.random.normal(jax.random.fold_in(jax.random.key(seed), 1), (8, 1024, 256), dtype=_x0.dtype)
    del _x0
    return _d

def reference(L0_attn_x, L0_attn_Wqkv, L0_attn_proj, L0_attn_Wout, L0_attn_bout, L0_ffn_Wg, L0_ffn_Ws1, L0_ffn_Ws3, L0_ffn_Ws2, L0_ffn_We1, L0_ffn_We3, L0_ffn_We2, L0_c, L0_wmod):

    def _L0_attn_ref(x, Wqkv, proj, Wout, bout):
        import jax, jax.numpy as jnp
        import numpy as np
        DIM = 256
        HEADS = 16
        HEAD_DIM = DIM // HEADS
        BLOCK = 32
        FEAT = 128
        EPS = 1e-08
        b, n, d = x.shape
        h, dh = (HEADS, HEAD_DIM)
        nb = n // BLOCK
        qkv = x @ Wqkv
        q, k, v = jnp.split(qkv, 3, axis=-1)

        def to_blocks(t):
            return t.reshape(b, nb, BLOCK, h, dh).transpose(0, 3, 1, 2, 4)
        q, k, v = (to_blocks(q), to_blocks(k), to_blocks(v))
        qf = jax.nn.elu(jnp.einsum('bhmsd,hdf->bhmsf', q, proj)) + 1.0
        kf = jax.nn.elu(jnp.einsum('bhmsd,hdf->bhmsf', k, proj)) + 1.0
        kv = jnp.einsum('bhmsf,bhmsd->bhmfd', kf, v)
        out = jnp.einsum('bhmsf,bhmfd->bhmsd', qf, kv)
        z = 1.0 / (jnp.einsum('bhmsf,bhmf->bhms', qf, kf.sum(axis=3)) + EPS)
        out = out * z[..., None]
        out = out.transpose(0, 2, 3, 1, 4).reshape(b, n, d)
        return out @ Wout + bout

    def _L0_ffn_ref(x, Wg, Ws1, Ws3, Ws2, We1, We3, We2):
        import jax, jax.numpy as jnp
        import numpy as np
        D_MODEL, FF_DIM = (256, 512)
        N_SHARED, N_ROUTED, TOP_K = (1, 8, 2)
        BATCH, SEQ = (2, 512)
        B, S, d = x.shape
        E = Wg.shape[1]
        xf = x.reshape(-1, d)
        T = xf.shape[0]
        gates = jax.nn.sigmoid(xf @ Wg)
        vals, idx = jax.lax.top_k(gates, TOP_K)
        vals = vals / vals.sum(axis=-1, keepdims=True)
        w = jnp.zeros((T, E), x.dtype).at[jnp.arange(T)[:, None], idx].add(vals)
        shared = jax.nn.silu(xf @ Ws1) * (xf @ Ws3) @ Ws2
        h = jax.nn.silu(jnp.einsum('td,edf->tef', xf, We1)) * jnp.einsum('td,edf->tef', xf, We3)
        routed = jnp.einsum('tef,efd,te->td', h, We2, w)
        out = (shared + routed) / (N_SHARED + TOP_K)
        return out.reshape(B, S, d)
    x = L0_attn_x
    mod = (_silu(L0_c) @ L0_wmod).reshape(L0_c.shape[0], 6, 1, -1)
    sa, ca, ga, sb, cb, gb = (mod[:, 0], mod[:, 1], mod[:, 2], mod[:, 3], mod[:, 4], mod[:, 5])
    ga = (2 * (ga >= 0) - 1) * jnp.maximum(jnp.abs(ga), 0.25)
    gb = (2 * (gb >= 0) - 1) * jnp.maximum(jnp.abs(gb), 0.25)
    h = _layernorm(x, axis=-1) * (1 + ca) + sa
    x = x + ga * _L0_attn_ref(h, L0_attn_Wqkv, L0_attn_proj, L0_attn_Wout, L0_attn_bout)
    h = _layernorm(x, axis=-1) * (1 + cb) + sb
    x = x + gb * _L0_ffn_ref(h, L0_ffn_Wg, L0_ffn_Ws1, L0_ffn_Ws3, L0_ffn_Ws2, L0_ffn_We1, L0_ffn_We3, L0_ffn_We2)
    return x

_drawn_inputs = setup_inputs


def setup_inputs(seed=0):
    import zlib

    import numpy as np

    out = dict(_drawn_inputs(seed))
    spreads = {'L0_attn_bout': (0.0, 0.332)}
    factors = {'L0_attn_proj': 8.0,
     'L0_ffn_Wg': 8.0,
     'L0_ffn_Ws1': 8.0,
     'L0_ffn_Ws3': 8.0,
     'L0_ffn_Ws2': 8.0,
     'L0_ffn_We1': 8.0,
     'L0_ffn_We3': 8.0,
     'L0_ffn_We2': 8.0}
    for name, (base, spread) in spreads.items():
        noise = np.random.default_rng([zlib.crc32(name.encode()), seed]).standard_normal(out[name].shape)
        drawn = base * np.exp(spread * noise) if base else spread * noise
        out[name] = jnp.asarray(drawn.astype(out[name].dtype))
    for name, factor in factors.items():
        out[name] = (out[name] * factor).astype(out[name].dtype)
    return out
```

```python
from contextlib import ExitStack

import concourse.bass as bass
from concourse import mybir

F32 = mybir.dt.float32
F16 = mybir.dt.float16
I32 = mybir.dt.int32
ALU = mybir.AluOpType
ACT = mybir.ActivationFunctionType
AX = mybir.AxisListType.X

P = 128
EPS_LN = 1e-5
EPS_Z = 1e-8

PLAN = [("B.oT0", 2), ("B.oT1", 3), ("F.hT0", 4), ("F.hT1", 5), ("B.wo0", 6), ("B.wo1", 7),
        ("F.q0", 8), ("F.k0", 9), ("F.q1", 10), ("F.k1", 11), ("B.nT0", 12), ("B.nT1", 13),
        ("B.route", 14), ("F.v0", 14), ("F.v1", 15), ("B.rank", 15)]
SLOTS = [name for name, _ in PLAN]
FRONT = [s for s in SLOTS if s[0] == "F"]
BACK = [s for s in SLOTS if s[0] == "B"]


def adaln_kernel(nc, x, wqkv, proj, wout, bout, wg, wexp, c, wmod, out):
    T, D = x.shape
    NBATCH = c.shape[0]
    H, DH, FEAT = proj.shape
    NE = wg.shape[1]
    GT = 512
    NT = GT // P
    G = T // GT
    KC = D // P
    BLOCK = 32
    VW = DH + 1
    PAIRS = H // 2
    FF = 512
    EW = 3 * FF * D // P
    WCOLS = wexp.shape[1]
    WPIECE = WCOLS // (2 * G)
    WSCALE, HSCALE, GSCALE = 16.0, 16.0, 16.0
    GR = 256
    RT = GR // P
    FC = FF // P
    REGION = T + GR
    NG1 = 2 * T // GR + NE
    NG2 = T // GR
    DUMP = NE * REGION
    assert GT * 2 == T // NBATCH and G % 2 == 0 and NG1 % 2 == 0 and EW == 3072
    assert WCOLS == (NE + 1) * EW and WPIECE * 2 * G == WCOLS

    hx = nc.dram_tensor("h_by_expert", (DUMP + GR, 2 * D), F16).ap()
    hs = nc.dram_tensor("h_by_token", (T, 2 * D), F16).ap()
    x1d = nc.dram_tensor("x_after_attention", (T, D), F32).ap()
    yx = nc.dram_tensor("y_by_group", (NG1 * GR, D), F32).ap()
    modd = nc.dram_tensor("modulation_rows", (NBATCH, 5, D), F32).ap()

    ctx = ExitStack()
    with ctx:
        keep, phase = ExitStack(), ExitStack()
        ctx.enter_context(keep)

        def sb(name, shape, dt, stack=None):
            return (stack or phase).enter_context(nc.sbuf_tensor(name, shape, dt))

        def sem(name):
            return ctx.enter_context(nc.semaphore(name))

        whi = sb("whi", [P, WCOLS], F16, keep)
        wlo = sb("wlo", [P, WCOLS], F16, keep)
        gate_w = sb("gate_w", [P, T // P, 2], F32, keep)
        row_all = sb("row_all", [P, T // P, 2], I32, keep)
        ident16 = sb("ident16", [P, P], F16, keep)
        zeros = sb("zeros", [P, 2 * D], F16, keep)
        small = sb("small", [P, 96], F32, keep)
        tab_e = sb("tab_e", [1, NG1], I32, keep)
        tab_r = sb("tab_r", [1, NG1], I32, keep)
        tab_z = sb("tab_z", [1, NE], I32, keep)
        cnt_i = sb("cnt_i", [P, 2, NE], I32, keep)

        wq_sb = sb("wq_sb", [P, KC, 3 * D], F32)
        wo_sb = sb("wo_sb", [P, KC, D], F32)
        wg_sb = sb("wg_sb", [P, KC, NE], F32)
        pst = sb("pst", [P, H, FEAT], F16)
        xin = sb("xin", [P, NT, D], F32)
        hT = sb("hT", [P, KC, GT], F32)
        qk = sb("qk", [P, 4, 2, GT], F16)
        stk = sb("stk", [P, 2, PAIRS, GT], F16)
        v_sb = sb("v_sb", [P, 2, NT, H, VW], F32)
        feat = sb("feat", [P, 4, GT], F32)
        att = sb("att", [P, 2, GT], F32)
        o_sb = sb("o_sb", [P, H, NT, VW], F32)
        on = sb("on", [P, NT, D], F32)
        tT = sb("tT", [P, KC, GT], F32)
        x1 = sb("x1", [P, NT, D], F32)
        mod = sb("mod", [P, 4, D], F32)
        hl = sb("hl", [P, NT, 2 * D], F16)
        wst = sb("wst", [P, WPIECE], F32)
        mask = sb("mask", [P, P], F32)
        ident = sb("ident", [P, P], F32)
        tri = sb("tri", [P, P], F16)
        ones16 = sb("ones16", [P, P], F16)
        modT = sb("modT", [P, 2, KC, NBATCH], F32)
        st6 = sb("st6", [P, 2, NT, 6], F32)
        mv = sb("mv", [P, 2, NT, 2], F32)
        rstd = sb("rstd", [P, 2, NT, 2], F32)
        vn = sb("vn", [P, 2, NT, 2], F32)
        half_ = sb("minus_half", [P, NT], F32)
        rden = sb("rden", [P, H * NT], F32)
        gate = sb("gate", [P, NT, NE], F32)
        cmp_ = sb("cmp", [P, NT, NE], F32)
        oh = sb("oh", [P, 2, NT, NE], F32)
        ohs = sb("ohs", [P, NT, NE], F16)
        top = sb("top", [P, 2, NT], F32)
        key = sb("key", [P, 2, NT], F32)
        wsum = sb("wsum", [P, NT], F32)
        pos = sb("pos", [P, 2, NT + 1, NE], F32)
        rowf = sb("rowf", [P, NT, 2], F32)
        row_now = sb("row_now", [P, NT, 2], I32)
        rev = sb("rev", [P, NE], F32)

        wmod_sb = stk[:, :, :, :].rearrange("p a b c -> p (a b c)").bitcast(F32)[:, 0:KC * 6 * D] \
            .rearrange("p (c n) -> p c n", c=KC)
        m8 = qk[0:NBATCH, :, :, :].rearrange("p a b c -> p (a b c)").bitcast(F32) \
            .rearrange("p (r n) -> p r n", n=D)
        rows8 = o_sb[0:NBATCH, :, :, :].rearrange("p a b c -> p (a b c)")[:, 0:4 * D] \
            .rearrange("p (r n) -> p r n", n=D)
        gb8 = on[0:NBATCH, 0, :]
        bout8 = on[0:NBATCH, 1, :]
        c_sb = on[0:NBATCH, 2, :]
        cT = rden[:, 0:KC * NBATCH].rearrange("p (c b) -> p c b", c=KC)
        pj = xin[0:DH, :, :].rearrange("p a b -> p (a b)")
        pj2 = x1[0:DH, :, :].rearrange("p a b -> p (a b)")
        halves = [hl[0:DH, :, :].rearrange("p a b -> p (a b)"),
                  feat[0:DH, :, :].rearrange("p a b -> p (a b)").bitcast(F16)[:, 0:2 * 8 * FEAT]]
        iota_i = row_all[:, 0:NE, :].rearrange("p a b -> p (a b)")

        tab = stk[:, :, :, :].rearrange("p a b c -> p (a b c)").bitcast(F32)

        phase.close()
        ph2 = ExitStack()
        hrow = sb("hrow", [P, 2, RT, 2 * D], F16, ph2)
        hTr = sb("hTr", [P, 2, 2 * KC, GR], F16, ph2)
        sil = sb("sil", [P, 2, 2, GR], F32, ph2)
        g32 = sb("g32", [P, 2, 2, GR], F32, ph2)
        ghi = sb("ghi", [P, 2, FC, GR], F16, ph2)
        glo = sb("glo", [P, 2, FC, GR], F16, ph2)
        ysb = sb("ysb", [P, 2, RT, D], F32, ph2)
        gy = sb("gy", [P, 2, RT, 2, D], F32, ph2)
        acc = sb("acc", [P, 2, RT, D], F32, ph2)
        x1b = sb("x1b", [P, 2, RT, D], F32, ph2)
        row_cur = sb("row_cur", [P, 2, RT * 2], I32, ph2)
        gb_sb = sb("gb_sb", [P, NBATCH, D], F32, ph2)
        ph2.close()

        ps = ctx.enter_context(nc.psum_tensor("ps", [P, 8, 512], F32))
        misc = ps[:, 7, :]
        feat_bank = lambda h, k: 2 if k else h % 2

        names = [
            "consts_ready", "pst_cleared", "weights_in", "proj_hi", "proj_lo", "cT_psum", "cT_ready",
            "mod_psum", "mod_chain", "mod_rows", "modT_psum", "modT_ready", "stk_ones", "prep_stored",
            "x_loaded", "stats_chain", "moments1", "moments2", "pow1_done", "pow2_done", "rstd1_ready", "rstd2_ready", "xn_ready", "misc_filled", "misc_drained", "qk_hi",
            "stack0_loaded", "stack1_loaded",
            "feat_psum", "exp_ready", "feat_ready", "scores_done", "att_ready", "av_done", "o_copied",
            "den_chain", "on_ready", "xres_loaded", "mod_loaded", "xres_ready", "xg_ready", "x1_ready",
            "x1_stored", "stats2_chain", "z_ready", "zmul_ready", "h2_ready", "hi_ready", "hl_ready",
            "hl_stored", "gate_exp", "route_chain", "rank_chain", "rows_ready", "scattered",
            "w_loaded", "w_scaled", "w_hi", "w_lo",
            "table_chain", "table_ready", "zero_filled", "hrow0_loaded", "hrow1_loaded", "tr_filled", "hT_ready",
            "ab_filled", "silu_ready", "g_ready", "ghi_ready", "glo_ready", "y_filled", "y_copied",
            "y_stored", "ysb_free", "rowcur_ready", "gathered", "x1b_loaded", "gb_loaded", "comb_chain",
            "acc_ready", "out_stored"]
        S = {n: sem(n) for n in names}
        hrow_loaded = [S["hrow0_loaded"], S["hrow1_loaded"]]
        stack_loaded = [S["stack0_loaded"], S["stack1_loaded"]]

        def use(step, what):
            if isinstance(step, int):
                if step == -1:
                    return FRONT.index(what)
                if step == 0:
                    return len(FRONT) + FRONT.index(what)
                if step == G - 1:
                    return 16 * (G - 1) + BACK.index(what)
                if step == G:
                    return 16 * (G - 1) + len(BACK) + BACK.index(what)
            return 16 * step + SLOTS.index(what)

        ROUTE, ONEHOT = 18, 14

        USES = 16 * (G - 1) + 2 * len(BACK)

        def steps(eng, step):
            step(0, 0, False, True, 0, 0)
            with eng.Fori(0, (G - 2) // 2) as i:
                step(i * 2 + 1, 1, True, True, i, i + 1)
                step(i * 2 + 2, 0, True, True, i, i + 1)
            step(G - 1, 1, True, False, NBATCH - 1, None)

        def group_steps(eng, first, count, step):
            step(first, first // 2, 0, 0, True, False)
            with eng.Fori(0, (count - 2) // 2) as i:
                step(i * 2 + (1 + first), i + first // 2, i * 2 + 1, 1, False, False)
                step(i * 2 + (2 + first), i + (first // 2 + 1), i * 2 + 2, 0, False, False)
            step(first + count - 1, (first + count) // 2 - 1, count - 1, 1, False, True)

        def wait_apart(eng, s, value):
            if not isinstance(value, int):
                value = eng.to_reg(value)
            eng.wait_ge(S["consts_ready"], 1)
            eng.wait_ge(s, value)

        def after_phase_a(eng):
            eng.wait_ge(S["av_done"], G * H)
            eng.wait_ge(S["o_copied"], G * PAIRS)
            eng.wait_ge(S["misc_drained"], USES)
            eng.wait_ge(S["scattered"], 16 * 2 * NT * G)
            eng.wait_ge(S["hl_stored"], 16 * G)
            eng.wait_ge(S["x1_stored"], 16 * G)
            eng.wait_ge(S["w_lo"], 2 * G)
            eng.wait_ge(S["table_ready"], 1)

        block = ctx.enter_context(nc.Block())

        @block.sync
        def _(sp):
            for dst, src in ((wmod_sb, wmod.rearrange("(c p) n -> p c n", p=P)),
                             (c_sb, c), (bout8, bout.rearrange("(a n) -> a n", a=1)[0, :].partition_broadcast(NBATCH)),
                             (pj, proj[0:H // 2].rearrange("h d f -> d h f")),
                             (pj2, proj[H // 2:H].rearrange("h d f -> d h f")),
                             (wq_sb[:, :, :], wqkv.rearrange("(c p) n -> p c n", p=P)),
                             (wo_sb[:, :, :], wout.rearrange("(c p) n -> p c n", p=P)),
                             (wg_sb[:, :, :], wg.rearrange("(c p) n -> p c n", p=P))):
                if len(dst.shape) == 2 and len(src.shape) == 3:
                    dst = dst.rearrange("d (h f) -> d h f", f=FEAT)
                sp.dma_start(dst, src).then_inc(S["weights_in"], 16)
            sp.wait_ge(S["pst_cleared"], 1)
            for half in range(2):
                sp.wait_ge(S["proj_lo"], half + 1)
                src = halves[half].rearrange("d (w h f) -> d w h f", w=2, f=FEAT)
                for hp in range(2):
                    for lane, w in ((0, 0), (2, 0), (4, 1)):
                        r = DH * (lane + hp)
                        sp.dma_start(pst[r:r + DH, half * 8 + hp:half * 8 + 8:2, :],
                                     src[:, w, hp:8:2, :]).then_inc(S["prep_stored"], 16)
            sp.wait_ge(S["mod_rows"], 1)
            sp.dma_start(modd[:, 0:4, :], rows8).then_inc(S["prep_stored"], 16)
            sp.dma_start(modd[:, 4, :], gb8).then_inc(S["prep_stored"], 16)
            sp.wait_ge(S["prep_stored"], 14 * 16)

            def load_x(f):
                sp.dma_start(xin[:, :, :], x[bass.ds(f * GT, GT), :].rearrange("(t p) d -> p t d", p=P)) \
                    .then_inc(S["x_loaded"], 16)

            def load_weights(s, r):
                sp.dma_start(wst[:, :], wexp[:, bass.ds(s * (2 * WPIECE) + r * WPIECE, WPIECE)]) \
                    .then_inc(S["w_loaded"], 16)

            def load_stack(g, ch):
                wait_apart(sp, S["misc_drained"], use(g, f"F.k{ch}") + 1)
                for a in range(4):
                    for r, w in ((0, 0), (1, 1), (2, 0)):
                        sp.dma_start(stk[32 * r:32 * r + 32, :, 4 * ch + a, :],
                                     qk[32 * a:32 * a + 32, 2 * ch:2 * ch + 2, w, :]) \
                            .then_inc(stack_loaded[ch], 16)

            def back_loads(b, batch):
                sp.dma_start(x1[:, :, :], x[bass.ds(b * GT, GT), :].rearrange("(t p) d -> p t d", p=P)) \
                    .then_inc(S["xres_loaded"], 16)
                sp.dma_start(mod[:, :, :].rearrange("p r d -> p (r d)"),
                             modd[bass.ds(batch, 1), 0:4, :].rearrange("a r d -> a (r d)")
                             .to_broadcast([P, 4 * D])).then_inc(S["mod_loaded"], 16)

            def store_x1(b):
                wait_apart(sp, S["x1_ready"], 2 * b + 2)
                sp.dma_start(x1d[bass.ds(b * GT, GT), :].rearrange("(t p) d -> p t d", p=P), x1[:, :, :]) \
                    .then_inc(S["x1_stored"], 16)

            def store_hl(b):
                wait_apart(sp, S["hl_ready"], 2 * b + 2)
                sp.dma_start(hs[bass.ds(b * GT, GT), :].rearrange("(t p) d -> p t d", p=P), hl[:, :, :]) \
                    .then_inc(S["hl_stored"], 16)

            def step(g, par, back, front, batch, _):
                if front:
                    load_x(g + 1)
                if back:
                    back_loads(g - 1, batch)
                wait_apart(sp, S["w_lo"], 2 * g + 1)
                load_weights(g, 1)
                if back:
                    store_x1(g - 1)
                if front:
                    wait_apart(sp, S["feat_psum"], g * 32 + 16)
                    load_stack(g, 0)
                    wait_apart(sp, S["feat_psum"], g * 32 + 32)
                    load_stack(g, 1)
                    wait_apart(sp, S["w_lo"], 2 * g + 2)
                    load_weights(g + 1, 0)
                if back:
                    store_hl(g - 1)
                    wait_apart(sp, S["x1_stored"], 16 * g)
                if front:
                    wait_apart(sp, S["misc_drained"], use(g, "F.hT1") + 1)

            load_x(0)
            load_weights(0, 0)
            sp.wait_ge(S["stk_ones"], 1)
            load_stack(-1, 0)
            load_stack(-1, 1)
            wait_apart(sp, S["misc_drained"], use(-1, "F.hT1") + 1)
            steps(sp, step)
            back_loads(G - 1, NBATCH - 1)
            store_x1(G - 1)
            store_hl(G - 1)

            sp.wait_ge(S["table_ready"], 1)
            for e in range(NE):
                row = sp.value_load(tab_z[0:1, e:e + 1], min_val=0, max_val=DUMP - GR)
                sp.dma_start(hx[bass.ds(row, GR), :].rearrange("(t p) d -> p t d", p=P),
                             zeros[:, :].unsqueeze(1).to_broadcast([P, RT, 2 * D])).then_inc(S["zero_filled"], 16)
            sp.dma_start(hx[DUMP:DUMP + GR, :].rearrange("(t p) d -> p t d", p=P),
                         zeros[:, :].unsqueeze(1).to_broadcast([P, RT, 2 * D])).then_inc(S["zero_filled"], 16)
            after_phase_a(sp)
            sp.wait_ge(S["zero_filled"], 16 * (NE + 1))
            sp.dma_start(gb_sb[:, :, :], modd[:, 4, :].partition_broadcast(P)).then_inc(S["gb_loaded"], 16)

            def load_rows(j, loc, par, first, routed):
                if not (routed and first):
                    wait_apart(sp, S["tr_filled"], j - 1)
                if routed:
                    row = sp.value_load(tab_r[0:1, bass.ds(loc, 1)], min_val=0, max_val=DUMP)
                    src = hx[bass.ds(row, GR), :]
                else:
                    src = hs[bass.ds(loc * GR, GR), :]
                sp.dma_start(hrow[:, par, :, :], src.rearrange("(t p) d -> p t d", p=P)) \
                    .then_inc(hrow_loaded[par], 16)

            def routed_loads(j, j2, loc, par, first, last):
                if not last:
                    load_rows(j + 1, loc + 1, 1 - par, first, True)

            load_rows(0, 0, 0, True, True)
            group_steps(sp, 0, NG1, routed_loads)

            def shared_loads(j, j2, loc, par, first, last):
                if not last:
                    load_rows(j + 1, loc + 1, 1 - par, False, False)

            load_rows(NG1, 0, 0, False, False)
            group_steps(sp, NG1, NG2, shared_loads)

        @block.gpsimd
        def _(pool):
            pool.memset(ident[:, :], 0.0)
            pool.memset(ident16[:, :], 0.0)
            pool.memset(tri[:, :], 1.0)
            pool.memset(mask[:, :], 1.0)
            pool.memset(ones16[:, :], 1.0)
            pool.memset(zeros[:, :], 0.0)
            pool.memset(small[:, 0:1], -1.0)
            pool.memset(half_[:, :], -0.5)
            pool.memset(v_sb[:, :, :, :, :], 1.0)
            pool.memset(pst[:, :, :], 0.0).then_inc(S["consts_ready"], 1)
            pool.wait_ge(S["consts_ready"], 1)
            pool.memset(pst[96:97, :, :], 1.0).then_inc(S["pst_cleared"], 1)
            pool.wait_ge(S["pst_cleared"], 1)
            for m in (ident, ident16):
                pool.affine_select(out=m[:, :], in_=m[:, :], compare_op=ALU.not_equal, fill=1.0, base=0,
                                   pattern=[[-1, P]], channel_multiplier=1)
            pool.affine_select(out=tri[:, :], in_=tri[:, :], compare_op=ALU.is_gt, fill=0.0, base=0,
                               pattern=[[1, P]], channel_multiplier=-1)
            mv4 = mask[:, :].rearrange("p (a b) -> p a b", b=BLOCK)
            pool.affine_select(out=mv4, in_=mv4, compare_op=ALU.is_ge, fill=0.0, base=0,
                               pattern=[[-BLOCK, P // BLOCK], [0, BLOCK]],
                               channel_multiplier=1).then_inc(S["consts_ready"], 1)
            pool.wait_ge(S["consts_ready"], 2)
            pool.affine_select(out=mv4, in_=mv4, compare_op=ALU.is_ge, fill=0.0, base=BLOCK - 1,
                               pattern=[[BLOCK, P // BLOCK], [0, BLOCK]], channel_multiplier=-1)
            pool.iota(iota_i[:, 0:NE], pattern=[[REGION, NE]], base=0, channel_multiplier=0)
            pool.iota(iota_i[:, NE:2 * NE], pattern=[[-1, NE]], base=NE, channel_multiplier=0)
            pool.iota(tab_r[0:1, :], pattern=[[1, NG1]], base=0, channel_multiplier=0) \
                .then_inc(S["consts_ready"], 1)
            pool.wait_ge(S["consts_ready"], 3)
            pool.tensor_copy(pos[:, 1, NT, :], iota_i[:, 0:NE])
            pool.tensor_copy(rev[:, :], iota_i[:, NE:2 * NE]).then_inc(S["consts_ready"], 1)
            pool.wait_ge(S["mod_psum"], 1)
            pool.memset(stk[96:P, :, :, :], 1.0).then_inc(S["stk_ones"], 1)
            pool.wait_ge(S["stk_ones"], 1)

            def inverse_std(which, t0, t1, n):
                k = which + 1
                pool.wait_ge(S[f"moments{k}"], n)
                pool.tensor_tensor(rstd[:, which, t0:t1, 0], vn[:, which, t0:t1, 0], half_[:, t0:t1], ALU.pow) \
                    .then_inc(S[f"pow{k}_done"], 1)
                pool.wait_ge(S[f"pow{k}_done"], n)
                pool.tensor_tensor(rstd[:, which, t0:t1, 1], rstd[:, which, t0:t1, 0], vn[:, which, t0:t1, 1],
                                   ALU.mult).then_inc(S[f"rstd{k}_ready"], 1)

            def split_weights(g, r):
                pool.wait_ge(S["w_hi"], 2 * g + r + 1)
                at = bass.ds(g * (2 * WPIECE) + r * WPIECE, WPIECE)
                pool.tensor_tensor(wlo[:, at], wst[:, :], whi[:, at], ALU.subtract).then_inc(S["w_lo"], 1)

            def finish_rows(b):
                pool.wait_ge(S["xres_loaded"], 16 * b + 16)
                pool.wait_ge(S["mod_loaded"], 16 * b + 16)
                pool.tensor_tensor(x1[:, :, :], x1[:, :, :], mod[:, 1:2, :].to_broadcast([P, NT, D]), ALU.add) \
                    .then_inc(S["xres_ready"], 1)
                for hf in range(2):
                    inverse_std(1, 2 * hf, 2 * hf + 2, 2 * b + hf + 1)
                for hf in range(2):
                    rows = on[:, 2 * hf:2 * hf + 2, :]
                    pool.wait_ge(S["z_ready"], 2 * b + hf + 1)
                    pool.tensor_tensor(rows, rows, mod[:, 2:3, :].to_broadcast([P, 2, D]), ALU.mult) \
                        .then_inc(S["zmul_ready"], 1)
                    pool.wait_ge(S["zmul_ready"], 2 * b + hf + 1)
                    pool.tensor_tensor(rows, rows, mod[:, 3:4, :].to_broadcast([P, 2, D]), ALU.add) \
                        .then_inc(S["h2_ready"], 1)
                for hf in range(2):
                    t = slice(2 * hf, 2 * hf + 2)
                    pool.wait_ge(S["hi_ready"], 2 * b + hf + 1)
                    pool.tensor_tensor(hl[:, t, D:2 * D], on[:, t, :], hl[:, t, 0:D], ALU.subtract) \
                        .then_inc(S["hl_ready"], 1)

            def scatter_rows(b):
                wait_apart(pool, S["rows_ready"], b + 1)
                wait_apart(pool, S["hl_ready"], 2 * b + 2)
                for t in range(NT):
                    for k in range(2):
                        pool.indirect_dma_start(
                            out=hx, out_offset=bass.IndirectOffsetOnAxis(ap=row_now[:, t, k:k + 1], axis=0),
                            in_=hl[:, t, :], in_offset=None).then_inc(S["scattered"], 16)
                pool.wait_ge(S["scattered"], 16 * 2 * NT * (b + 1))
                pool.wait_ge(S["hl_stored"], 16 * (b + 1))

            def step(g, par, back, front, *_):
                if front:
                    inverse_std(0, 0, NT, g + 2)
                split_weights(g, 0)
                if back:
                    finish_rows(g - 1)
                split_weights(g, 1)
                if back:
                    scatter_rows(g - 1)

            inverse_std(0, 0, NT, 1)
            steps(pool, step)
            finish_rows(G - 1)
            scatter_rows(G - 1)

            after_phase_a(pool)
            for n in range(2):
                pool.memset(small[:, 1:2], 0.0).then_inc(S["ysb_free"], 1)
                pool.wait_ge(S["ysb_free"], n + 1)

            def store_y(j, loc, par):
                pool.wait_ge(S["y_copied"], j + 1)
                pool.dma_start(yx[bass.ds(loc * GR, GR), :].rearrange("(t p) d -> p t d", p=P), ysb[:, par, :, :]) \
                    .then_inc(S["y_stored"], 16)
                wait_apart(pool, S["y_stored"], 16 * j + 16)
                pool.memset(small[:, 1:2], 0.0).then_inc(S["ysb_free"], 1)
                pool.wait_ge(S["ysb_free"], j + 3)

            def routed(j, j2, loc, par, first, last):
                if not first:
                    store_y(j - 1, loc - 1, 1 - par)
                if last:
                    store_y(j, loc, par)

            group_steps(pool, 0, NG1, routed)
            pool.wait_ge(S["y_stored"], 16 * NG1)

            def fetch(loc, par):
                pool.tensor_copy(row_cur[:, par, :],
                                 row_all[:, bass.ds(loc * RT, RT), :].rearrange("p t k -> p (t k)")) \
                    .then_inc(S["rowcur_ready"], 1)
                pool.dma_start(x1b[:, par, :, :], x1d[bass.ds(loc * GR, GR), :]
                               .rearrange("(t p) d -> p t d", p=P)).then_inc(S["x1b_loaded"], 16)
                wait_apart(pool, S["rowcur_ready"], loc + 1)
                for t in range(RT):
                    for k in range(2):
                        pool.indirect_dma_start(
                            out=gy[:, par, t, k, :], out_offset=None, in_=yx,
                            in_offset=bass.IndirectOffsetOnAxis(ap=row_cur[:, par, 2 * t + k:2 * t + k + 1], axis=0)
                        ).then_inc(S["gathered"], 16)

            def store_out(loc, par):
                pool.wait_ge(S["acc_ready"], loc + 1)
                pool.dma_start(out[bass.ds(loc * GR, GR), :].rearrange("(t p) d -> p t d", p=P), acc[:, par, :, :]) \
                    .then_inc(S["out_stored"], 16)

            def shared(j, j2, loc, par, first, last):
                if not first:
                    store_out(loc - 1, 1 - par)
                    pool.wait_ge(S["out_stored"], 16 * loc)
                if not last:
                    pool.wait_ge(S["gathered"], 64 * (loc + 1))
                    pool.wait_ge(S["x1b_loaded"], 16 * (loc + 1))
                    fetch(loc + 1, 1 - par)
                if last:
                    store_out(loc, par)

            fetch(0, 0)
            group_steps(pool, NG1, NG2, shared)
            pool.wait_ge(S["out_stored"], 16 * NG2)

        @block.scalar
        def _(act):
            act.wait_ge(S["weights_in"], 16 * 8)
            for half, src in enumerate((pj, pj2)):
                act.activation(halves[half][:, 0:8 * FEAT], src, ACT.Copy).then_inc(S["proj_hi"], 1)
            act.wait_ge(S["cT_psum"], 1)
            act.activation(cT, misc[:, 0:KC * NBATCH].rearrange("p (c b) -> p c b", c=KC), ACT.Silu) \
                .then_inc(S["cT_ready"], 1)
            act.wait_ge(S["modT_psum"], 1)
            act.activation(modT[:, :, :, :].rearrange("p a b c -> p (a b c)"),
                           misc[:, 0:2 * KC * NBATCH], ACT.Copy).then_inc(S["modT_ready"], 1)
            act.wait_ge(S["modT_ready"], 1)
            act.wait_ge(S["prep_stored"], 14 * 16)

            def xn(f):
                act.wait_ge(S["rstd1_ready"], f + 1)
                for t in range(NT):
                    ins = act.activation(xin[:, t, :], xin[:, t, :], ACT.Identity,
                                         scale=rstd[:, 0, t, 0:1], bias=rstd[:, 0, t, 1:2])
                ins.then_inc(S["xn_ready"], 1)

            def read_scratch(s, what):
                wait_apart(act, S["misc_filled"], use(s, what) + 1)

            def front_piece(s, what, batch, vpar):
                read_scratch(s, what)
                if what[:4] == "F.hT":
                    cc = int(what[4])
                    act.activation(hT[:, cc, :], misc, ACT.Identity,
                                   scale=modT[:, 1, cc, bass.ds(batch, 1)], bias=modT[:, 0, cc, bass.ds(batch, 1)]) \
                        .then_inc(S["misc_drained"], 1)
                elif what[:3] == "F.v":
                    tp = int(what[3])
                    act.activation(v_sb[:, vpar, 2 * tp:2 * tp + 2, :, 0:DH].rearrange("p t h d -> p (t h) d"),
                                   misc.rearrange("p (t d) -> p t d", d=DH), ACT.Copy) \
                        .then_inc(S["misc_drained"], 1)
                else:
                    jj = ["F.q0", "F.k0", "F.q1", "F.k1"].index(what)
                    if not (isinstance(s, int) and s < 0):
                        act.wait_ge(stack_loaded[jj // 2], 16 * 12 * (s + 1))
                    act.activation(qk[:, jj, 0, :], misc, ACT.Copy).then_inc(S["qk_hi"], 1)

            def back_piece(s, what):
                if what[:4] in ("B.oT", "B.nT"):
                    read_scratch(s, what)
                    act.activation(tT[:, int(what[4]), :], misc, ACT.Copy).then_inc(S["misc_drained"], 1)
                elif what == "B.route":
                    read_scratch(s, what)
                    act.activation(gate[:, :, :].rearrange("p t e -> p (t e)"), misc[:, 0:NT * NE], ACT.Exp,
                                   scale=-1.0 / HSCALE).then_inc(S["misc_drained"], 1)

            def z(b, hf):
                act.wait_ge(S["rstd2_ready"], 2 * b + hf + 1)
                for t in (2 * hf, 2 * hf + 1):
                    ins = act.activation(on[:, t, :], x1[:, t, :], ACT.Identity,
                                         scale=rstd[:, 1, t, 0:1], bias=rstd[:, 1, t, 1:2])
                ins.then_inc(S["z_ready"], 1)

            def hi(b, hf):
                act.wait_ge(S["h2_ready"], 2 * b + hf + 1)
                act.activation(hl[:, 2 * hf:2 * hf + 2, 0:D], on[:, 2 * hf:2 * hf + 2, :], ACT.Copy) \
                    .then_inc(S["hi_ready"], 1)

            def exps(g, h):
                for k in range(2):
                    b = 2 * (h % 2) + k
                    act.wait_ge(S["feat_psum"], 32 * g + 2 * h + k + 1)
                    if k == 0 and not (isinstance(g, int) and g == 0 and h < 2):
                        act.wait_ge(S["scores_done"], 16 * g + h - 1)
                    act.activation(feat[:, b, :], ps[:, feat_bank(h, k), :], ACT.Exp, bias=small[:, 0:1]) \
                        .then_inc(S["exp_ready"], 1)

            def copy_o(g, pair):
                act.wait_ge(S["av_done"], 16 * g + 2 * pair + 2)
                act.activation(o_sb[:, 2 * pair:2 * pair + 2, :, :].rearrange("p h t v -> p (h t v)"),
                               ps[:, 5 + pair % 2, 0:2 * NT * VW], ACT.Copy).then_inc(S["o_copied"], 1)

            def weights(g, r):
                act.wait_ge(S["w_loaded"], 32 * g + 16 * r + 16)
                act.activation(wst[:, :], wst[:, :], ACT.Copy, scale=WSCALE).then_inc(S["w_scaled"], 1)
                act.wait_ge(S["w_scaled"], 2 * g + r + 1)
                act.activation(whi[:, bass.ds(g * (2 * WPIECE) + r * WPIECE, WPIECE)], wst[:, :], ACT.Copy) \
                    .then_inc(S["w_hi"], 1)

            def step(g, par, back, front, batch_b, batch_f):
                for h in range(H):
                    if h < H - 1:
                        exps(g, h + 1)
                    elif front:
                        exps(g + 1, 0)
                    if h == 1:
                        weights(g, 0)
                    if front and h == 2:
                        xn(g + 1)
                    if h == 6:
                        weights(g, 1)
                    if back and h in (8, 9):
                        z(g - 1, h - 8)
                    if back and h in (10, 11):
                        hi(g - 1, h - 10)
                    for what, at in PLAN:
                        if at == h and what[0] == "F" and front:
                            front_piece(g, what, batch_f, 1 - par)
                        if at == h and what[0] == "B" and back:
                            back_piece(g, what)
                    if h % 2 == 0 and h:
                        copy_o(g, h // 2 - 1)
                    elif h == 0 and back:
                        copy_o(g - 1, PAIRS - 1)

            xn(0)
            for what in FRONT:
                front_piece(-1, what, 0, 0)
            exps(0, 0)
            steps(act, step)
            copy_o(G - 1, PAIRS - 1)
            for what in ("B.oT0", "B.oT1"):
                back_piece(G, what)
            z(G - 1, 0)
            z(G - 1, 1)
            hi(G - 1, 0)
            hi(G - 1, 1)
            for what in ("B.nT0", "B.nT1", "B.route"):
                back_piece(G, what)

            after_phase_a(act)

            def hidden(j, par):
                for hf in range(2):
                    act.wait_ge(S["ab_filled"], 2 * j + hf + 1)
                    act.activation(sil[:, hf, :, :], ps[:, 2 * hf, :].rearrange("p (c n) -> p c n", n=GR),
                                   ACT.Silu, scale=1.0 / (WSCALE * HSCALE)).then_inc(S["silu_ready"], 1)
                    act.wait_ge(S["g_ready"], 2 * j + hf + 1)
                    act.activation(ghi[:, par, 2 * hf:2 * hf + 2, :], g32[:, hf, :, :], ACT.Copy) \
                        .then_inc(S["ghi_ready"], 1)

            def copy_y(j, par):
                act.wait_ge(S["y_filled"], j + 1)
                act.wait_ge(S["ysb_free"], j + 1)
                act.activation(ysb[:, par, :, :], ps[:, 4 + par, :].rearrange("p (t d) -> p t d", d=D),
                               ACT.Copy).then_inc(S["y_copied"], 1)

            def routed(j, j2, loc, par, first, last):
                hidden(j, par)
                if not first:
                    copy_y(j - 1, 1 - par)
                if last:
                    copy_y(j, par)

            def shared(j, j2, loc, par, first, last):
                hidden(j, par)

            group_steps(act, 0, NG1, routed)
            group_steps(act, NG1, NG2, shared)

        @block.vector
        def _(dve):
            def chain(name, start=0):
                count = [start]

                def link(ins):
                    count[0] = count[0] + 1
                    ins.then_inc(S[name], 1)
                    wait_apart(dve, S[name], count[0])
                return link

            dve.wait_ge(S["weights_in"], 16 * 8)
            for half, src in enumerate((pj, pj2)):
                dve.wait_ge(S["proj_hi"], half + 1)
                dve.tensor_tensor(halves[half][:, 8 * FEAT:16 * FEAT], src, halves[half][:, 0:8 * FEAT],
                                  ALU.subtract).then_inc(S["proj_lo"], 1)
            dve.wait_ge(S["mod_psum"], 1)
            mp = ps[0:NBATCH, 0:3, :].rearrange("p a (b n) -> p (a b) n", n=D)
            link = chain("mod_chain")
            link(dve.tensor_copy(m8[:, 0, :], mp[:, 0, :]))
            link(dve.tensor_scalar(m8[:, 1, :], mp[:, 1, :], 1.0, None, ALU.add))
            link(dve.tensor_scalar(rows8[:, 2, :], mp[:, 4, :], 1.0, HSCALE, ALU.add, ALU.mult))
            link(dve.tensor_scalar(rows8[:, 3, :], mp[:, 3, :], HSCALE, None, ALU.mult))
            for n, dst in ((2, rows8[:, 0, :]), (5, gb8)):
                link(dve.tensor_scalar(m8[:, 2, :], mp[:, n, :], 0.0, 2.0, ALU.is_ge, ALU.mult))
                link(dve.tensor_scalar(m8[:, 2, :], m8[:, 2, :], 1.0, None, ALU.subtract))
                link(dve.tensor_scalar(m8[:, 3, :], mp[:, n, :], -1.0, None, ALU.mult))
                link(dve.tensor_tensor(m8[:, 3, :], m8[:, 3, :], mp[:, n, :], ALU.max))
                link(dve.tensor_scalar(m8[:, 3, :], m8[:, 3, :], 0.25, None, ALU.max))
                link(dve.tensor_tensor(dst, m8[:, 2, :], m8[:, 3, :], ALU.mult))
            link(dve.tensor_tensor(rows8[:, 1, :], rows8[:, 0, :], bout8, ALU.mult))
            dve.tensor_scalar(gb8, gb8, 1.0 / (3.0 * GSCALE * WSCALE), None, ALU.mult) \
                .then_inc(S["mod_rows"], 1)

            def stats(src, which, tiles, link):
                t0, t1 = tiles[0], tiles[-1] + 1
                for t in tiles:
                    ins = dve.bn_stats(st6[:, which, t, :], src[:, t, :])
                link(ins)
                for t in tiles:
                    ins = dve.bn_aggr(mv[:, which, t, :], st6[:, which, t, :])
                link(ins)
                dve.tensor_scalar(vn[:, which, t0:t1, 0], mv[:, which, t0:t1, 1], EPS_LN, None, ALU.add)
                ins = dve.tensor_scalar(vn[:, which, t0:t1, 1], mv[:, which, t0:t1, 0], -1.0, None, ALU.mult)
                ins.then_inc(S[("moments1", "moments2")[which]], 1)

            def front_stats(f):
                dve.wait_ge(S["x_loaded"], 16 * f + 16)
                if not (isinstance(f, int) and f == 0):
                    dve.wait_ge(S["xn_ready"], f)
                stats(xin, 0, range(NT), chain("stats_chain", 2 * f))

            def lo(s, what):
                jj = ["F.q0", "F.k0", "F.q1", "F.k1"].index(what)
                dve.wait_ge(S["qk_hi"], 4 * (s + 1) + jj + 1)
                dve.tensor_tensor(qk[:, jj, 1, :], misc, qk[:, jj, 0, :], ALU.subtract) \
                    .then_inc(S["misc_drained"], 1)

            def features(g, h):
                for k in range(2):
                    b = 2 * (h % 2) + k
                    dve.wait_ge(S["exp_ready"], 32 * g + 2 * h + k + 1)
                    dve.scalar_tensor_tensor(feat[:, b, :], feat[:, b, :], 1.0, ps[:, feat_bank(h, k), :], ALU.min, ALU.max) \
                        .then_inc(S["feat_ready"], 1)

            def mask_scores(g, h):
                dve.wait_ge(S["scores_done"], 16 * g + h + 1)
                if not (isinstance(g, int) and g == 0 and h < 2):
                    dve.wait_ge(S["av_done"], 16 * g + h - 1)
                dve.tensor_tensor(att[:, h % 2, :].rearrange("p (t q) -> p t q", t=NT),
                                  ps[:, 3 + h % 2, :].rearrange("p (t q) -> p t q", t=NT),
                                  mask[:, :].unsqueeze(1).to_broadcast([P, NT, P]), ALU.mult) \
                    .then_inc(S["att_ready"], 1)

            def normalise(b):
                dve.wait_ge(S["o_copied"], PAIRS * b + PAIRS)
                dve.wait_ge(S["xres_ready"], b + 1)
                link = chain("den_chain", 2 * b)
                den = rden[:, :].rearrange("p (h t) -> p h t", t=NT)
                link(dve.tensor_scalar(den, o_sb[:, :, :, DH], EPS_Z, None, ALU.add))
                link(dve.reciprocal(rden[:, :], rden[:, :]))
                for t in range(NT):
                    ins = dve.tensor_tensor(on[:, t, :].rearrange("p (h d) -> p h d", d=DH), o_sb[:, :, t, 0:DH],
                                            den[:, :, t].unsqueeze(2).to_broadcast([P, H, DH]), ALU.mult)
                ins.then_inc(S["on_ready"], 1)

            def residual(b, s, hf):
                dve.wait_ge(S["misc_filled"], use(s, f"B.wo{hf}") + 1)
                xg = on[:, 2 * hf:2 * hf + 2, :]
                dve.tensor_tensor(xg, misc.rearrange("p (t d) -> p t d", d=D),
                                  mod[:, 0:1, :].to_broadcast([P, 2, D]), ALU.mult).then_inc(S["misc_drained"], 1)
                dve.wait_ge(S["misc_drained"], use(s, f"B.wo{hf}") + 1)
                rows = x1[:, 2 * hf:2 * hf + 2, :]
                dve.tensor_tensor(rows, rows, xg, ALU.add).then_inc(S["x1_ready"], 1)

            def stats2(b, hf):
                dve.wait_ge(S["x1_ready"], 2 * b + hf + 1)
                stats(x1, 1, range(2 * hf, 2 * hf + 2), chain("stats2_chain", 4 * b + 2 * hf))

            def route(b, s):
                dve.wait_ge(S["misc_drained"], use(s, "B.route") + 1)
                link = chain("route_chain", ROUTE * b)
                three = lambda v: v.unsqueeze(2).to_broadcast([P, NT, NE])
                revb = rev[:, :].unsqueeze(1).to_broadcast([P, NT, NE])
                link(dve.tensor_scalar(gate[:, :, :], gate[:, :, :], 1.0, None, ALU.add))
                link(dve.reciprocal(gate[:, :, :], gate[:, :, :]))
                for k in range(2):
                    link(dve.tensor_reduce(top[:, k, :], gate[:, :, :], AX, ALU.max))
                    link(dve.tensor_tensor(cmp_[:, :, :], gate[:, :, :], three(top[:, k, :]), ALU.is_equal))
                    link(dve.tensor_tensor(cmp_[:, :, :], cmp_[:, :, :], revb, ALU.mult))
                    link(dve.tensor_reduce(key[:, k, :], cmp_[:, :, :], AX, ALU.max))
                    link(dve.tensor_tensor(oh[:, k, :, :], revb, three(key[:, k, :]), ALU.is_equal))
                    if k == 0:
                        link(dve.scalar_tensor_tensor(gate[:, :, :], oh[:, 0, :, :], -2.0, gate[:, :, :],
                                                      ALU.mult, ALU.add))
                link(dve.tensor_tensor(ohs[:, :, :], oh[:, 0, :, :], oh[:, 1, :, :], ALU.add))
                link(dve.tensor_tensor(wsum[:, :], top[:, 0, :], top[:, 1, :], ALU.add))
                link(dve.reciprocal(wsum[:, :], wsum[:, :]))
                tiles = bass.ds(b * NT, NT)
                link(dve.tensor_tensor(gate_w[:, tiles, 0], top[:, 0, :], wsum[:, :], ALU.mult))
                link(dve.tensor_tensor(gate_w[:, tiles, 1], top[:, 1, :], wsum[:, :], ALU.mult))

            def rank(b, s, par):
                dve.wait_ge(S["misc_filled"], use(s, "B.rank") + 1)
                link = chain("rank_chain", 5 * b)
                dve.tensor_tensor(pos[:, par, :, :], misc[:, 0:(NT + 1) * NE].rearrange("p (t e) -> p t e", e=NE),
                                  pos[:, 1 - par, NT:NT + 1, :].to_broadcast([P, NT + 1, NE]), ALU.add) \
                    .then_inc(S["misc_drained"], 1)
                dve.wait_ge(S["misc_drained"], use(s, "B.rank") + 1)
                for k in range(2):
                    link(dve.tensor_tensor(oh[:, k, :, :], oh[:, k, :, :], pos[:, par, 0:NT, :], ALU.mult))
                    link(dve.tensor_reduce(rowf[:, :, k], oh[:, k, :, :], AX, ALU.add))
                link(dve.tensor_copy(row_all[:, bass.ds(b * NT, NT), :], rowf[:, :, :]))
                dve.tensor_copy(row_now[:, :, :], rowf[:, :, :]).then_inc(S["rows_ready"], 1)

            def step(g, par, back, front, *_):
                for h in range(H):
                    if h < H - 1:
                        features(g, h + 1)
                    elif front:
                        features(g + 1, 0)
                    mask_scores(g, h)
                    if front and h == 1:
                        front_stats(g + 1)
                    for what, at in PLAN:
                        if front and at == h and what[:3] in ("F.q", "F.k"):
                            lo(g, what)
                    if back:
                        if h == 1:
                            normalise(g - 1)
                        if h in (6, 7):
                            residual(g - 1, g, h - 6)
                            stats2(g - 1, h - 6)
                        if h == 14:
                            route(g - 1, g)
                        if h == 15:
                            rank(g - 1, g, 1 - par)

            dve.wait_ge(S["modT_psum"], 1)
            front_stats(0)
            for what in ("F.q0", "F.k0", "F.q1", "F.k1"):
                lo(-1, what)
            features(0, 0)
            steps(dve, step)
            b = G - 1
            normalise(b)
            for hf in range(2):
                residual(b, G, hf)
                stats2(b, hf)
            route(b, G)
            rank(b, G, 1)

            link = chain("table_chain")
            fin = pos[:, 1, NT, :]
            cols = lambda n: tab[0:1, n * NG1:(n + 1) * NG1]
            jj, ex, first_, row, off, ok = (cols(n) for n in range(6))
            big = tab[:, 8 * NG1:8 * NG1 + 4 * NE]
            start, ng, cum, shift = (big[:, n * NE:(n + 1) * NE] for n in range(4))
            cube = tab[0:1, 16 * NG1:16 * NG1 + NG1 * NE].rearrange("p (j e) -> p j e", e=NE)
            rows = tab[:, 25 * NG1:25 * NG1 + 2 * T // P]
            over = tab[:, 28 * NG1:28 * NG1 + 2 * T // P]
            link(dve.tensor_copy(tab_z[0:1, :], fin[0:1, :]))
            link(dve.tensor_copy(jj, tab_r[0:1, :]))
            link(dve.tensor_scalar(start, rev[:, :], -float(REGION), float(REGION * NE), ALU.mult, ALU.add))
            link(dve.scalar_tensor_tensor(ng, fin, float(GR - 1), start, ALU.add, ALU.subtract))
            link(dve.tensor_copy(cnt_i[:, 0, :], ng))
            link(dve.tensor_scalar(cnt_i[:, 1, :], cnt_i[:, 0, :], GR.bit_length() - 1, None,
                                   ALU.arith_shift_right))
            link(dve.tensor_copy(ng, cnt_i[:, 1, :]))
            link(dve.tensor_scalar(shift, ng, float(GR), float(REGION), ALU.mult, ALU.subtract))
            link(dve.tensor_copy(rows, row_all[:, :, :].rearrange("p t k -> p (t k)")))
            for e in range(1, NE):
                link(dve.tensor_scalar(over, row_all[:, :, :].rearrange("p t k -> p (t k)"), float(e * REGION), None, ALU.is_ge))
                link(dve.scalar_tensor_tensor(rows, over, shift[:, e - 1:e], rows, ALU.mult, ALU.add))
            link(dve.tensor_copy(row_all[:, :, :].rearrange("p t k -> p (t k)"), rows))
            start, ng, cum = start[0:1, :], ng[0:1, :], cum[0:1, :]
            link(dve.memset(start, 1.0))
            link(dve.tensor_tensor_scan(cum, start, ng, 0.0, ALU.mult, ALU.add))
            link(dve.tensor_tensor(cube, jj.unsqueeze(2).to_broadcast([1, NG1, NE]),
                                   cum.unsqueeze(1).to_broadcast([1, NG1, NE]), ALU.is_ge))
            link(dve.tensor_reduce(ex, cube, AX, ALU.add))
            link(dve.tensor_tensor(cube, cube, ng.unsqueeze(1).to_broadcast([1, NG1, NE]), ALU.mult))
            link(dve.tensor_reduce(first_, cube, AX, ALU.add))
            link(dve.tensor_scalar(ok, ex, NE - 0.5, None, ALU.is_le))
            link(dve.tensor_tensor(off, jj, first_, ALU.subtract))
            link(dve.tensor_scalar(off, off, float(GR), None, ALU.mult))
            link(dve.scalar_tensor_tensor(row, ex, float(REGION), off, ALU.mult, ALU.add))
            link(dve.tensor_scalar(off, row, float(DUMP), None, ALU.subtract))
            link(dve.tensor_tensor(off, off, ok, ALU.mult))
            link(dve.tensor_scalar(off, off, float(DUMP), None, ALU.add))
            link(dve.tensor_copy(tab_r[0:1, :], off))
            link(dve.tensor_scalar(ex, ex, float(NE - 1), None, ALU.min))
            link(dve.tensor_scalar(ex, ex, 1.0, float(EW), ALU.add, ALU.mult))
            dve.tensor_copy(tab_e[0:1, :], ex).then_inc(S["table_ready"], 1)
            after_phase_a(dve)

            def copy_hT(j, par):
                dve.wait_ge(S["tr_filled"], j + 1)
                dve.tensor_copy(hTr[:, par, :, :].rearrange("p c n -> p (c n)"), ps[:, 6, :].bitcast(F16)) \
                    .then_inc(S["hT_ready"], 1)

            def hidden(j, par, first, last):
                if not last:
                    copy_hT(j + 1, 1 - par)
                for hf in range(2):
                    dve.wait_ge(S["silu_ready"], 2 * j + hf + 1)
                    dve.scalar_tensor_tensor(g32[:, hf, :, :].rearrange("p c n -> p (c n)"), ps[:, 2 * hf + 1, :],
                                             GSCALE / (WSCALE * HSCALE),
                                             sil[:, hf, :, :].rearrange("p c n -> p (c n)"), ALU.mult, ALU.mult) \
                        .then_inc(S["g_ready"], 1)
                    dve.wait_ge(S["ghi_ready"], 2 * j + hf + 1)
                    dve.tensor_tensor(glo[:, par, 2 * hf:2 * hf + 2, :], g32[:, hf, :, :],
                                      ghi[:, par, 2 * hf:2 * hf + 2, :], ALU.subtract).then_inc(S["glo_ready"], 1)

            def routed(j, j2, loc, par, first, last):
                hidden(j, par, first, last)

            def combine(j, loc, par, batch):
                dve.wait_ge(S["y_filled"], j + 1)
                dve.wait_ge(S["gathered"], 64 * loc + 64)
                dve.wait_ge(S["x1b_loaded"], 16 * loc + 16)
                link = chain("comb_chain", 3 * loc)
                w = lambda t, k: gate_w[:, bass.ds(loc * RT + t, 1), k]
                for t in range(RT):
                    ins = dve.scalar_tensor_tensor(acc[:, par, t, :], gy[:, par, t, 0, :], w(t, 0),
                                                   ps[:, 4 + par, t * D:(t + 1) * D], ALU.mult, ALU.add)
                link(ins)
                for t in range(RT):
                    ins = dve.scalar_tensor_tensor(acc[:, par, t, :], gy[:, par, t, 1, :], w(t, 1),
                                                   acc[:, par, t, :], ALU.mult, ALU.add)
                link(ins)
                link(dve.tensor_tensor(acc[:, par, :, :], acc[:, par, :, :],
                                       gb_sb[:, bass.ds(batch, 1), :].to_broadcast([P, RT, D]), ALU.mult))
                dve.tensor_tensor(acc[:, par, :, :], acc[:, par, :, :], x1b[:, par, :, :], ALU.add) \
                    .then_inc(S["acc_ready"], 1)

            PB = T // NBATCH // GR

            def shared(j, j2, loc, par, first, last):
                hidden(j, par, first, last)
                if not first:
                    combine(j - 1, loc - 1, 1 - par, (loc - 1) // PB)
                if last:
                    combine(j, loc, par, loc // PB)

            copy_hT(0, 0)
            group_steps(dve, 0, NG1, routed)
            copy_hT(NG1, 0)
            dve.wait_ge(S["gb_loaded"], 16)
            group_steps(dve, NG1, NG2, shared)

        @block.tensor
        def _(pe):
            pe.wait_ge(S["consts_ready"], 4)
            pe.wait_ge(S["weights_in"], 16 * 8)
            for cc in range(KC):
                ins = pe.transpose(misc[:, cc * NBATCH:(cc + 1) * NBATCH], c_sb[:, cc * P:(cc + 1) * P],
                                   ident[0:NBATCH, 0:NBATCH])
            ins.then_inc(S["cT_psum"], 1)
            pe.wait_ge(S["cT_ready"], 1)
            for n in range(3):
                for cc in range(KC):
                    ins = pe.matmul(ps[0:NBATCH, n, :], cT[:, cc, :], wmod_sb[:, cc, n * 512:(n + 1) * 512],
                                    start=(cc == 0), stop=(cc == KC - 1))
            ins.then_inc(S["mod_psum"], 1)
            pe.wait_ge(S["mod_rows"], 1)
            for r in range(2):
                for cc in range(KC):
                    at = (r * KC + cc) * NBATCH
                    ins = pe.transpose(misc[:, at:at + NBATCH], m8[:, r, cc * P:(cc + 1) * P],
                                       ident[0:NBATCH, 0:NBATCH])
            ins.then_inc(S["modT_psum"], 1)
            pe.wait_ge(S["modT_ready"], 1)

            def scratch(s, what):
                u = use(s, what)
                if not (isinstance(u, int) and u == 0):
                    pe.wait_ge(S["misc_drained"], u)

            def front_piece(s, what, vpar):
                scratch(s, what)
                if what[:4] == "F.hT":
                    cc = int(what[4])
                    pe.wait_ge(S["xn_ready"], s + 2)
                    for t in range(NT):
                        ins = pe.transpose(misc[:, t * P:(t + 1) * P], xin[:, t, cc * P:(cc + 1) * P], ident[:, :])
                elif what[:3] == "F.v":
                    for t in range(2):
                        for cc in range(KC):
                            tok = (2 * int(what[3]) + t) * P
                            ins = pe.matmul(misc[:, t * D:(t + 1) * D], hT[:, cc, tok:tok + P],
                                            wq_sb[:, cc, 2 * D:3 * D], start=(cc == 0), stop=(cc == KC - 1))
                else:
                    at = (0 if what[2] == "q" else D) + int(what[3]) * P
                    if what == "F.q0":
                        pe.wait_ge(S["misc_drained"], use(s, "F.hT1") + 1)
                    for cc in range(KC):
                        ins = pe.matmul(misc, wq_sb[:, cc, at:at + P], hT[:, cc, :],
                                        start=(cc == 0), stop=(cc == KC - 1))
                ins.then_inc(S["misc_filled"], 1)

            def back_piece(s, b, what):
                scratch(s, what)
                if what[:4] in ("B.oT", "B.nT"):
                    cc = int(what[4])
                    if what[2] == "o":
                        pe.wait_ge(S["on_ready"], b + 1)
                    else:
                        pe.wait_ge(S["h2_ready"], 2 * b + 2)
                    for t in range(NT):
                        ins = pe.transpose(misc[:, t * P:(t + 1) * P], on[:, t, cc * P:(cc + 1) * P], ident[:, :])
                elif what[:4] == "B.wo":
                    for t in range(2):
                        for cc in range(KC):
                            tok = (2 * int(what[4]) + t) * P
                            ins = pe.matmul(misc[:, t * D:(t + 1) * D], tT[:, cc, tok:tok + P], wo_sb[:, cc, :],
                                            start=(cc == 0), stop=(cc == KC - 1))
                elif what == "B.route":
                    for t in range(NT):
                        for cc in range(KC):
                            ins = pe.matmul(misc[:, t * NE:(t + 1) * NE], tT[:, cc, t * P:(t + 1) * P],
                                            wg_sb[:, cc, :], start=(cc == 0), stop=(cc == KC - 1))
                else:
                    pe.wait_ge(S["route_chain"], ROUTE * b + ONEHOT)
                    for t in range(NT):
                        pe.matmul(misc[:, (t + 1) * NE:(NT + 1) * NE].rearrange("p (t e) -> p t e", e=NE),
                                  ones16[:, :], ohs[:, t:t + 1, :].to_broadcast([P, NT - t, NE]),
                                  start=(t == 0), stop=(t == NT - 1), skip_group_check=True)
                    ins = pe.matmul(misc[:, 0:NT * NE], tri[:, :], ohs[:, :, :].rearrange("p t e -> p (t e)"),
                                    start=False, stop=True, skip_group_check=True)
                ins.then_inc(S["misc_filled"], 1)

            def features(g, h):
                if h == 0:
                    pe.wait_ge(S["stack0_loaded"], 192 * g + 192)
                if h == 8:
                    pe.wait_ge(S["stack1_loaded"], 192 * g + 192)
                for k in range(2):
                    if k == 0 and not (isinstance(g, int) and g == 0 and h < 2):
                        pe.wait_ge(S["feat_ready"], 32 * g + 2 * h - 2)
                    if k == 1 and not (isinstance(g, int) and g == 0 and h < 1):
                        pe.wait_ge(S["feat_ready"], 32 * g + 2 * h)
                    pe.matmul(ps[:, feat_bank(h, k), :], pst[:, h, :], stk[:, k, h // 2, :],
                              start=True, stop=True).then_inc(S["feat_psum"], 1)

            def scores(g, h):
                pe.wait_ge(S["feat_ready"], 32 * g + 2 * h + 2)
                if not (isinstance(g, int) and g == 0 and h < 2):
                    pe.wait_ge(S["att_ready"], 16 * g + h - 1)
                for t in range(NT):
                    tok = slice(t * P, (t + 1) * P)
                    ins = pe.matmul(ps[:, 3 + h % 2, tok], feat[:, 2 * (h % 2) + 1, tok],
                                    feat[:, 2 * (h % 2), tok], start=True, stop=True)
                ins.then_inc(S["scores_done"], 1)

            def weigh(g, h, par):
                pe.wait_ge(S["att_ready"], 16 * g + h + 1)
                pair = h // 2
                if h % 2 == 0 and not (isinstance(g, int) and g == 0 and pair < 2):
                    pe.wait_ge(S["o_copied"], PAIRS * g + pair - 1)
                for t in range(NT):
                    at = (h % 2) * NT * VW + t * VW
                    ins = pe.matmul(ps[:, 5 + pair % 2, at:at + VW], att[:, h % 2, t * P:(t + 1) * P], v_sb[:, par, t, h, :],
                                    start=True, stop=True)
                ins.then_inc(S["av_done"], 1)

            def step(g, par, back, front, *_):
                for h in range(H):
                    if h < H - 1:
                        features(g, h + 1)
                    elif front:
                        features(g + 1, 0)
                    scores(g, h)
                    for what, at in PLAN:
                        if at == h and what[0] == "F" and front:
                            front_piece(g, what, 1 - par)
                        if at == h and what[0] == "B" and back:
                            back_piece(g, g - 1, what)
                    if h:
                        weigh(g, h - 1, par)
                    elif back:
                        weigh(g - 1, H - 1, 1 - par)

            for what in FRONT:
                front_piece(-1, what, 0)
            pe.wait_ge(S["stk_ones"], 1)
            pe.wait_ge(S["misc_drained"], len(FRONT))
            features(0, 0)
            steps(pe, step)
            weigh(G - 1, H - 1, 1)
            for what in BACK:
                back_piece(G, G - 1, what)

            after_phase_a(pe)

            def turn(j, j2, par):
                pe.wait_ge(hrow_loaded[par], 16 * j2 + 16)
                if not (isinstance(j, int) and j == 0):
                    pe.wait_ge(S["hT_ready"], j)
                bank = ps[:, 6, :].bitcast(F16)
                for c4 in range(2 * KC):
                    for t in range(RT):
                        at = c4 * GR + t * P
                        ins = pe.transpose(bank[:, at:at + P], hrow[:, par, t, c4 * P:(c4 + 1) * P], ident16[:, :])
                ins.then_inc(S["tr_filled"], 1)

            def products(dst, pairs):
                for n, (w, h) in enumerate(pairs):
                    ins = pe.matmul(dst, w, h, start=(n == 0), stop=(n == len(pairs) - 1))
                return ins

            def up(j, par, col):
                pe.wait_ge(S["hT_ready"], j + 1)
                for hf in range(2):
                    if not (isinstance(j, int) and j == 0):
                        pe.wait_ge(S["g_ready"], 2 * j - 1 + hf)
                    for m in range(2):
                        for f in range(2):
                            def w(half, cc):
                                at = col + ((m * KC + cc) * FF + (2 * hf + f) * P)
                                return half[:, bass.ds(at, P)]
                            h = lambda lane, cc: hTr[:, par, lane * KC + cc, :]
                            ins = products(ps[:, 2 * hf + m, f * GR:(f + 1) * GR],
                                           [q for cc in range(KC) for q in
                                            ((w(whi, cc), h(0, cc)), (w(whi, cc), h(1, cc)), (w(wlo, cc), h(0, cc)))])
                    ins.then_inc(S["ab_filled"], 1)

            def down(j, par, col):
                pe.wait_ge(S["glo_ready"], 2 * j + 2)
                for t in range(RT):
                    g = lambda half, f: half[:, par, f, t * P:(t + 1) * P]
                    w = lambda half, f: half[:, bass.ds(col + (2 * KC * FF + f * D), D)]
                    ins = products(ps[:, 4 + par, t * D:(t + 1) * D],
                                   [q for f in range(FC) for q in
                                    ((g(ghi, f), w(whi, f)), (g(ghi, f), w(wlo, f)), (g(glo, f), w(whi, f)))])
                ins.then_inc(S["y_filled"], 1)

            def column(loc):
                return pe.value_load(tab_e[0:1, bass.ds(loc, 1)], min_val=EW, max_val=NE * EW)

            def routed(j, j2, loc, par, first, last):
                if not last:
                    turn(j + 1, j2 + par, 1 - par)
                up(j, par, column(loc))
                if not first:
                    down(j - 1, 1 - par, column(loc - 1))
                if last:
                    down(j, par, column(loc))

            def shared(j, j2, loc, par, first, last):
                if not last:
                    turn(j + 1, j2 + par, 1 - par)
                up(j, par, 0)
                if not first:
                    down(j - 1, 1 - par, 0)
                if last:
                    down(j, par, 0)

            turn(0, 0, 0)
            group_steps(pe, 0, NG1, routed)
            turn(NG1, NG1 // 2, 0)
            group_steps(pe, NG1, NG2, shared)


def _by_partition(w, chunk=128):
    n = w.shape[0] // chunk
    return w.reshape(n, chunk, w.shape[1]).transpose(1, 0, 2).reshape(chunk, -1)


def kernel(**inputs):
    import numpy as np
    import concourse.bacc as bacc
    from concourse.bass_utils import run_bass_kernel_spmd

    a = {k: np.asarray(v) for k, v in inputs.items()}
    experts = [(a["L0_ffn_Ws1"], a["L0_ffn_Ws3"], a["L0_ffn_Ws2"])]
    experts += [(a["L0_ffn_We1"][e], a["L0_ffn_We3"][e], a["L0_ffn_We2"][e])
                for e in range(a["L0_ffn_We1"].shape[0])]
    x = a["L0_attn_x"]
    arrays = {
        "x": x.reshape(-1, x.shape[-1]), "wqkv": a["L0_attn_Wqkv"], "proj": a["L0_attn_proj"],
        "wout": a["L0_attn_Wout"], "bout": a["L0_attn_bout"], "wg": a["L0_ffn_Wg"],
        "wexp": np.concatenate([_by_partition(w) for e in experts for w in e], axis=1),
        "c": a["L0_c"], "wmod": a["L0_wmod"],
    }
    arrays = {k: np.ascontiguousarray(v) for k, v in arrays.items()}
    nc = bacc.Bacc("TRN2", target_bir_lowering=False, num_devices=1)
    args = {k: nc.dram_tensor(f"in_{k}", v.shape, mybir.dt.from_np(v.dtype), kind="ExternalInput").ap()
            for k, v in arrays.items()}
    out = nc.dram_tensor("out", arrays["x"].shape, F32, kind="ExternalOutput").ap()
    adaln_kernel(nc, out=out, **args)
    r = run_bass_kernel_spmd(nc, [{f"in_{k}": v for k, v in arrays.items()}], core_ids=[0])
    return r.results[0]["out"].reshape(x.shape)
```

```python
from contextlib import ExitStack

import concourse.bass as bass
from concourse import mybir

F32 = mybir.dt.float32
F16 = mybir.dt.float16
I32 = mybir.dt.int32
ALU = mybir.AluOpType
ACT = mybir.ActivationFunctionType
AX = mybir.AxisListType.X

P = 128
EPS_LN = 1e-5
EPS_Z = 1e-8

PLAN = [("B.oT0", 2), ("B.oT1", 3), ("B.wo0", 4), ("B.wo1", 5), ("F.hT0", 5.5), ("F.hT1", 6),
        ("F.q0", 7), ("F.k0", 8), ("F.q1", 9), ("F.k1", 10), ("B.nT0", 10.5), ("B.nT1", 11),
        ("F.v0", 11.5), ("B.route", 12), ("F.v1", 13), ("B.rank", 15.5)]
SLOTS = [name for name, _ in PLAN]
FRONT = [s for s in SLOTS if s[0] == "F"]
BACK = [s for s in SLOTS if s[0] == "B"]


def adaln_kernel(nc, x, wqkv, proj, wout, bout, wg, wexp, c, wmod, out):
    T, D = x.shape
    NBATCH = c.shape[0]
    H, DH, FEAT = proj.shape
    NE = wg.shape[1]
    GT = 512
    NT = GT // P
    G = T // GT
    KC = D // P
    BLOCK = 32
    VW = DH + 1
    PAIRS = H // 2
    FF = 512
    EW = 3 * FF * D // P
    WCOLS = wexp.shape[1]
    WPIECE = WCOLS // (2 * G)
    WSCALE, HSCALE, GSCALE = 16.0, 16.0, 16.0
    GR = 256
    RT = GR // P
    FC = FF // P
    REGION = T + GR
    NG1 = 2 * T // GR + NE
    NG2 = T // GR
    DUMP = NE * REGION
    assert GT * 2 == T // NBATCH and G % 2 == 0 and NG1 % 2 == 0 and EW == 3072
    assert WCOLS == (NE + 1) * EW and WPIECE * 2 * G == WCOLS

    hx = nc.dram_tensor("h_by_expert", (DUMP + GR, 2 * D), F16).ap()
    hs = nc.dram_tensor("h_by_token", (T, 2 * D), F16).ap()
    x1d = nc.dram_tensor("x_after_attention", (T, D), F32).ap()
    yx = nc.dram_tensor("y_by_group", (NG1 * GR, D), F32).ap()
    modd = nc.dram_tensor("modulation_rows", (NBATCH, 5, D), F32).ap()

    ctx = ExitStack()
    with ctx:
        keep, phase = ExitStack(), ExitStack()
        ctx.enter_context(keep)

        def sb(name, shape, dt, stack=None):
            return (stack or phase).enter_context(nc.sbuf_tensor(name, shape, dt))

        def sem(name):
            return ctx.enter_context(nc.semaphore(name))

        whi = sb("whi", [P, WCOLS], F16, keep)
        wlo = sb("wlo", [P, WCOLS], F16, keep)
        gate_w = sb("gate_w", [P, T // P, 2], F32, keep)
        row_all = sb("row_all", [P, T // P, 2], I32, keep)
        ident16 = sb("ident16", [P, P], F16, keep)
        zeros = sb("zeros", [P, 2 * D], F16, keep)
        small = sb("small", [P, 16], F32, keep)
        tab_e = sb("tab_e", [1, NG1], I32, keep)
        tab_r = sb("tab_r", [1, NG1], I32, keep)
        tab_z = sb("tab_z", [1, NE], I32, keep)
        cnt_i = sb("cnt_i", [P, 2, NE], I32, keep)

        wq_sb = sb("wq_sb", [P, 2, KC, 3 * D], F16)
        wo_sb = sb("wo_sb", [P, KC, D], F32)
        wg_sb = sb("wg_sb", [P, KC, NE], F32)
        pst = sb("pst", [P, H, FEAT], F16)
        xin = sb("xin", [P, NT, D], F32)
        hT = sb("hT", [P, 2, KC, GT], F16)
        qk = sb("qk", [P, 4, 2, GT], F16)
        stk = sb("stk", [P, 2, PAIRS, GT], F16)
        v_sb = sb("v_sb", [P, 2, NT, H, VW], F32)
        feat = sb("feat", [P, 4, GT], F32)
        att = sb("att", [P, 2, GT], F32)
        o_sb = sb("o_sb", [P, H, NT, VW], F32)
        on = sb("on", [P, NT, D], F32)
        tT = sb("tT", [P, KC, GT], F32)
        x1 = sb("x1", [P, NT, D], F32)
        mod = sb("mod", [P, 4, D], F32)
        hl = sb("hl", [P, NT, 2 * D], F16)
        wst = sb("wst", [P, WPIECE], F32)
        mask = sb("mask", [P, P], F32)
        ident = sb("ident", [P, P], F32)
        tri = sb("tri", [P, P], F16)
        ones16 = sb("ones16", [P, P], F16)
        modT = sb("modT", [P, 2, KC, NBATCH], F32)
        st6 = sb("st6", [P, 2, NT, 6], F32)
        mv = sb("mv", [P, 2, NT, 2], F32)
        rstd = sb("rstd", [P, 2, NT, 2], F32)
        vn = sb("vn", [P, 2, NT, 2], F32)
        half_ = sb("minus_half", [P, NT], F32)
        rden = sb("rden", [P, H * NT], F32)
        gate = sb("gate", [P, NT, NE], F32)
        cmp_ = sb("cmp", [P, NT, NE], F32)
        oh = sb("oh", [P, 2, NT, NE], F32)
        ohs = sb("ohs", [P, NT, NE], F16)
        top = sb("top", [P, 2, NT], F32)
        key = sb("key", [P, 2, NT], F32)
        wsum = sb("wsum", [P, NT], F32)
        pos = sb("pos", [P, 2, NT + 1, NE], F32)
        rowf = sb("rowf", [P, NT, 2], F32)
        row_now = sb("row_now", [P, NT, 2], I32)
        rev = sb("rev", [P, NE], F32)

        wmod_sb = stk[:, :, :, :].rearrange("p a b c -> p (a b c)").bitcast(F32)[:, 0:KC * 6 * D] \
            .rearrange("p (c n) -> p c n", c=KC)
        m8 = qk[0:NBATCH, :, :, :].rearrange("p a b c -> p (a b c)").bitcast(F32) \
            .rearrange("p (r n) -> p r n", n=D)
        rows8 = o_sb[0:NBATCH, :, :, :].rearrange("p a b c -> p (a b c)")[:, 0:4 * D] \
            .rearrange("p (r n) -> p r n", n=D)
        gb8 = on[0:NBATCH, 0, :]
        bout8 = on[0:NBATCH, 1, :]
        c_sb = on[0:NBATCH, 2, :]
        cT = rden[:, 0:KC * NBATCH].rearrange("p (c b) -> p c b", c=KC)
        pj = xin[0:DH, :, :].rearrange("p a b -> p (a b)")
        pj2 = x1[0:DH, :, :].rearrange("p a b -> p (a b)")
        halves = [hl[0:DH, :, :].rearrange("p a b -> p (a b)"),
                  feat[0:DH, :, :].rearrange("p a b -> p (a b)").bitcast(F16)[:, 0:2 * 8 * FEAT]]
        wq_in = [tT[:, :, :].rearrange("p c n -> p (c n)")[:, 0:3 * D],
                 hT[:, :, :, :].rearrange("p a c n -> p (a c n)").bitcast(F32)[:, 0:3 * D]]
        iota_i = row_all[:, 0:NE, :].rearrange("p a b -> p (a b)")

        tab = stk[:, :, :, :].rearrange("p a b c -> p (a b c)").bitcast(F32)

        phase.close()
        ph2 = ExitStack()
        hrow = sb("hrow", [P, 2, RT, 2 * D], F16, ph2)
        hTr = sb("hTr", [P, 2, 2 * KC, GR], F16, ph2)
        sil = sb("sil", [P, 2, 2, GR], F32, ph2)
        g32 = sb("g32", [P, 2, 2, 2, GR], F32, ph2)
        ghi = sb("ghi", [P, 2, FC, GR], F16, ph2)
        glo = sb("glo", [P, 2, FC, GR], F16, ph2)
        ysb = sb("ysb", [P, 2, RT, D], F32, ph2)
        gy = sb("gy", [P, 2, RT, 2, D], F32, ph2)
        acc = sb("acc", [P, 2, RT, D], F32, ph2)
        x1b = sb("x1b", [P, 2, RT, D], F32, ph2)
        row_cur = sb("row_cur", [P, 2, RT * 2], I32, ph2)
        gb_sb = sb("gb_sb", [P, NBATCH, D], F32, ph2)
        rows_f = sb("rows_f", [P, 2, 2 * T // P], F32, ph2)
        ph2.close()

        ps = ctx.enter_context(nc.psum_tensor("ps", [P, 8, 512], F32))
        misc = ps[:, 7, :]
        AHEAD, OW = 3, 512 // (2 * NT)
        first_of = lambda h: min(h, H - AHEAD)
        feat_bank = lambda h, k: (6, 2)[h % 2] if k else h % 2

        names = [
            "consts_ready", "pst_cleared", "weights_in", "wq_hi", "wq_lo", "hT_lo", "proj_hi", "proj_lo", "cT_psum", "cT_ready",
            "mod_psum", "mod_chain", "mod_rows", "modT_psum", "modT_ready", "stk_ones", "prep_stored",
            "x_loaded", "stats_chain", "moments1", "moments2", "pow1_done", "pow2_done", "rstd1_ready", "rstd2_ready", "xn_ready", "misc_filled", "misc_drained", "qk_hi",
            "stack0_loaded", "stack1_loaded",
            "feat_psum", "exp_ready", "feat_ready", "scores_done", "att_ready", "av_done", "o_copied",
            "den_chain", "on_ready", "xres_loaded", "mod_loaded", "xres_ready", "x1_ready",
            "x1_stored", "stats2_chain", "z_ready", "zmul_ready", "h2_ready", "hi_ready", "hl_ready",
            "hl_stored", "route_chain", "rank_chain", "rows_ready", "scattered",
            "w_loaded", "w_scaled", "w_hi", "w_lo",
            "table_chain", "row_chain", "rows_moved", "table_ready", "rests_ready", "zero_filled", "hrow0_loaded", "hrow1_loaded", "tr_filled", "hT_ready",
            "ab_filled", "silu_ready", "g_ready", "ghi_ready", "glo_ready", "y_filled", "y_copied",
            "y_stored", "ysb_free", "rowcur_ready", "gathered", "x1b_loaded", "gb_loaded", "comb_chain",
            "acc_ready", "out0_stored", "out1_stored"]
        S = {n: sem(n) for n in names}
        out_stored = [S["out0_stored"], S["out1_stored"]]
        hrow_loaded = [S["hrow0_loaded"], S["hrow1_loaded"]]
        stack_loaded = [S["stack0_loaded"], S["stack1_loaded"]]

        def use(step, what):
            if isinstance(step, int):
                if step == -1:
                    return FRONT.index(what)
                if step == 0:
                    return len(FRONT) + FRONT.index(what)
                if step == G - 1:
                    return 16 * (G - 1) + BACK.index(what)
                if step == G:
                    return 16 * (G - 1) + len(BACK) + BACK.index(what)
            return 16 * step + SLOTS.index(what)

        ROUTE, ONEHOT, PARTS = 18, 14, 9

        USES = 16 * (G - 1) + 2 * len(BACK)

        def steps(eng, step):
            step(0, 0, False, True, 0, 0)
            with eng.Fori(0, (G - 2) // 2) as i:
                step(i * 2 + 1, 1, True, True, i, i + 1)
                step(i * 2 + 2, 0, True, True, i, i + 1)
            step(G - 1, 1, True, False, NBATCH - 1, None)

        def group_steps(eng, first, count, step):
            step(first, first // 2, 0, 0, True, False)
            with eng.Fori(0, (count - 2) // 2) as i:
                step(i * 2 + (1 + first), i + first // 2, i * 2 + 1, 1, False, False)
                step(i * 2 + (2 + first), i + (first // 2 + 1), i * 2 + 2, 0, False, False)
            step(first + count - 1, (first + count) // 2 - 1, count - 1, 1, False, True)

        def wait_apart(eng, s, value):
            if not isinstance(value, int):
                value = eng.to_reg(value)
            eng.wait_ge(S["consts_ready"], 1)
            eng.wait_ge(s, value)

        def after_phase_a(eng):
            eng.wait_ge(S["av_done"], G * H)
            eng.wait_ge(S["o_copied"], G * PAIRS)
            eng.wait_ge(S["misc_drained"], USES)
            eng.wait_ge(S["scattered"], 16 * 2 * NT * G)
            eng.wait_ge(S["hl_stored"], 16 * G)
            eng.wait_ge(S["x1_stored"], 16 * G)
            eng.wait_ge(S["w_lo"], 2 * G)
            eng.wait_ge(S["table_ready"], 1)

        block = ctx.enter_context(nc.Block())

        @block.sync
        def _(sp):
            for dst, src in ((wmod_sb, wmod.rearrange("(c p) n -> p c n", p=P)),
                             (c_sb, c), (bout8, bout.rearrange("(a n) -> a n", a=1)[0, :].partition_broadcast(NBATCH)),
                             (pj, proj[0:H // 2].rearrange("h d f -> d h f")),
                             (pj2, proj[H // 2:H].rearrange("h d f -> d h f")),
                             (wq_in[0], wqkv[0:P, :]), (wq_in[1], wqkv[P:2 * P, :]),
                             (wo_sb[:, :, :], wout.rearrange("(c p) n -> p c n", p=P)),
                             (wg_sb[:, :, :], wg.rearrange("(c p) n -> p c n", p=P))):
                if len(dst.shape) == 2 and len(src.shape) == 3:
                    dst = dst.rearrange("d (h f) -> d h f", f=FEAT)
                sp.dma_start(dst, src).then_inc(S["weights_in"], 16)
            sp.wait_ge(S["pst_cleared"], 1)
            for half in range(2):
                sp.wait_ge(S["proj_lo"], half + 1)
                src = halves[half].rearrange("d (w h f) -> d w h f", w=2, f=FEAT)
                for hp in range(2):
                    for lane, w in ((0, 0), (2, 0), (4, 1)):
                        r = DH * (lane + hp)
                        sp.dma_start(pst[r:r + DH, half * 8 + hp:half * 8 + 8:2, :],
                                     src[:, w, hp:8:2, :]).then_inc(S["prep_stored"], 16)
            sp.wait_ge(S["mod_rows"], 1)
            sp.dma_start(modd[:, 0:4, :], rows8).then_inc(S["prep_stored"], 16)
            sp.dma_start(modd[:, 4, :], gb8).then_inc(S["prep_stored"], 16)
            sp.wait_ge(S["prep_stored"], 14 * 16)

            def load_weights(s, r):
                sp.dma_start(wst[:, :], wexp[:, bass.ds(s * (2 * WPIECE) + r * WPIECE, WPIECE)]) \
                    .then_inc(S["w_loaded"], 16)

            def load_stack(g, ch):
                wait_apart(sp, S["misc_drained"], use(g, f"F.k{ch}") + 1)
                for a in range(4):
                    for r, w in ((0, 0), (1, 1), (2, 0)):
                        sp.dma_start(stk[32 * r:32 * r + 32, :, 4 * ch + a, :],
                                     qk[32 * a:32 * a + 32, 2 * ch:2 * ch + 2, w, :]) \
                            .then_inc(stack_loaded[ch], 16)

            def back_loads(b, batch):
                sp.dma_start(x1[:, :, :], x[bass.ds(b * GT, GT), :].rearrange("(t p) d -> p t d", p=P)) \
                    .then_inc(S["xres_loaded"], 16)
                sp.dma_start(mod[:, :, :].rearrange("p r d -> p (r d)"),
                             modd[bass.ds(batch, 1), 0:4, :].rearrange("a r d -> a (r d)")
                             .to_broadcast([P, 4 * D])).then_inc(S["mod_loaded"], 16)

            def store_x1(b):
                wait_apart(sp, S["x1_ready"], 2 * b + 2)
                sp.dma_start(x1d[bass.ds(b * GT, GT), :].rearrange("(t p) d -> p t d", p=P), x1[:, :, :]) \
                    .then_inc(S["x1_stored"], 16)

            def store_hl(b):
                wait_apart(sp, S["hl_ready"], 2 * b + 3)
                sp.dma_start(hs[bass.ds(b * GT, GT), :].rearrange("(t p) d -> p t d", p=P), hl[:, :, :]) \
                    .then_inc(S["hl_stored"], 16)

            def step(g, par, back, front, batch, _):
                if back:
                    back_loads(g - 1, batch)
                wait_apart(sp, S["w_lo"], 2 * g + 1)
                load_weights(g, 1)
                if back:
                    store_x1(g - 1)
                if front:
                    wait_apart(sp, S["feat_psum"], g * 32 + 16)
                    load_stack(g, 0)
                if back:
                    store_hl(g - 1)
                if front:
                    wait_apart(sp, S["feat_psum"], g * 32 + 32)
                    load_stack(g, 1)
                    wait_apart(sp, S["w_lo"], 2 * g + 2)
                    load_weights(g + 1, 0)
                if back:
                    wait_apart(sp, S["x1_stored"], 16 * g)
                    wait_apart(sp, S["hl_stored"], 16 * g)

            load_weights(0, 0)
            sp.wait_ge(S["stk_ones"], 1)
            load_stack(-1, 0)
            load_stack(-1, 1)
            steps(sp, step)
            back_loads(G - 1, NBATCH - 1)
            store_x1(G - 1)
            store_hl(G - 1)

            sp.wait_ge(S["rests_ready"], 1)
            for e in range(NE):
                row = sp.value_load(tab_z[0:1, e:e + 1], min_val=0, max_val=DUMP - GR)
                sp.dma_start(hx[bass.ds(row, GR), :].rearrange("(t p) d -> p t d", p=P),
                             zeros[:, :].unsqueeze(1).to_broadcast([P, RT, 2 * D])).then_inc(S["zero_filled"], 16)
            sp.dma_start(hx[DUMP:DUMP + GR, :].rearrange("(t p) d -> p t d", p=P),
                         zeros[:, :].unsqueeze(1).to_broadcast([P, RT, 2 * D])).then_inc(S["zero_filled"], 16)
            after_phase_a(sp)
            sp.wait_ge(S["zero_filled"], 16 * (NE + 1))
            def load_rows(j, loc, par, first, routed):
                if not (routed and first):
                    wait_apart(sp, S["tr_filled"], j - 1)
                if routed:
                    row = sp.value_load(tab_r[0:1, bass.ds(loc, 1)], min_val=0, max_val=DUMP)
                    src = hx[bass.ds(row, GR), :]
                else:
                    src = hs[bass.ds(loc * GR, GR), :]
                sp.dma_start(hrow[:, par, :, :], src.rearrange("(t p) d -> p t d", p=P)) \
                    .then_inc(hrow_loaded[par], 16)

            def routed_loads(j, j2, loc, par, first, last):
                if not last:
                    load_rows(j + 1, loc + 1, 1 - par, first, True)
                else:
                    load_rows(NG1, 0, 0, False, False)

            load_rows(0, 0, 0, True, True)
            sp.dma_start(gb_sb[:, :, :], modd[:, 4, :].partition_broadcast(P)).then_inc(S["gb_loaded"], 16)
            group_steps(sp, 0, NG1, routed_loads)

            def shared_loads(j, j2, loc, par, first, last):
                if not last:
                    load_rows(j + 1, loc + 1, 1 - par, False, False)

            group_steps(sp, NG1, NG2, shared_loads)

        @block.gpsimd
        def _(pool):
            pool.memset(small[:, 5:6], 0.0).then_inc(S["hl_ready"], 1)
            pool.memset(ident[:, :], 0.0)
            pool.memset(ident16[:, :], 0.0)
            pool.memset(tri[:, :], 1.0)
            pool.memset(mask[:, :], 1.0)
            pool.memset(ones16[:, :], 1.0)
            pool.memset(zeros[:, :], 0.0)
            pool.memset(small[:, 0:1], -1.0)
            pool.memset(half_[:, :], -0.5)
            pool.memset(v_sb[:, :, :, :, :], 1.0)
            pool.memset(pst[:, :, :], 0.0).then_inc(S["consts_ready"], 1)
            pool.wait_ge(S["consts_ready"], 1)
            pool.memset(pst[96:97, :, :], 1.0).then_inc(S["pst_cleared"], 1)
            pool.wait_ge(S["pst_cleared"], 1)
            for m in (ident, ident16):
                pool.affine_select(out=m[:, :], in_=m[:, :], compare_op=ALU.not_equal, fill=1.0, base=0,
                                   pattern=[[-1, P]], channel_multiplier=1)
            pool.affine_select(out=tri[:, :], in_=tri[:, :], compare_op=ALU.is_gt, fill=0.0, base=0,
                               pattern=[[1, P]], channel_multiplier=-1)
            mv4 = mask[:, :].rearrange("p (a b) -> p a b", b=BLOCK)
            pool.affine_select(out=mv4, in_=mv4, compare_op=ALU.is_ge, fill=0.0, base=0,
                               pattern=[[-BLOCK, P // BLOCK], [0, BLOCK]],
                               channel_multiplier=1).then_inc(S["consts_ready"], 1)
            pool.wait_ge(S["consts_ready"], 2)
            pool.affine_select(out=mv4, in_=mv4, compare_op=ALU.is_ge, fill=0.0, base=BLOCK - 1,
                               pattern=[[BLOCK, P // BLOCK], [0, BLOCK]], channel_multiplier=-1)
            pool.iota(iota_i[:, 0:NE], pattern=[[REGION, NE]], base=0, channel_multiplier=0)
            pool.iota(iota_i[:, NE:2 * NE], pattern=[[-1, NE]], base=NE, channel_multiplier=0)
            pool.iota(tab_r[0:1, :], pattern=[[1, NG1]], base=0, channel_multiplier=0) \
                .then_inc(S["consts_ready"], 1)
            pool.wait_ge(S["consts_ready"], 3)
            pool.tensor_copy(pos[:, 1, NT, :], iota_i[:, 0:NE])
            pool.tensor_copy(rev[:, :], iota_i[:, NE:2 * NE]).then_inc(S["consts_ready"], 1)
            def inverse_std(which, t0, t1, n):
                k = which + 1
                pool.wait_ge(S[f"moments{k}"], n)
                pool.tensor_tensor(rstd[:, which, t0:t1, 0], vn[:, which, t0:t1, 0], half_[:, t0:t1], ALU.pow) \
                    .then_inc(S[f"pow{k}_done"], 1)
                pool.wait_ge(S[f"pow{k}_done"], n)
                pool.tensor_tensor(rstd[:, which, t0:t1, 1], rstd[:, which, t0:t1, 0], vn[:, which, t0:t1, 1],
                                   ALU.mult).then_inc(S[f"rstd{k}_ready"], 1)

            inverse_std(0, 0, NT, 1)
            pool.wait_ge(S["rstd1_ready"], 1)
            pool.wait_ge(S["mod_psum"], 1)
            pool.memset(stk[96:P, :, :, :], 1.0).then_inc(S["stk_ones"], 1)
            pool.wait_ge(S["stk_ones"], 1)

            def split_weights(g, r):
                pool.wait_ge(S["w_hi"], 2 * g + r + 1)
                at = bass.ds(g * (2 * WPIECE) + r * WPIECE, WPIECE)
                pool.tensor_tensor(wlo[:, at], wst[:, :], whi[:, at], ALU.subtract).then_inc(S["w_lo"], 1)

            def residual_rows(b):
                pool.wait_ge(S["xres_loaded"], 16 * b + 16)
                pool.wait_ge(S["mod_loaded"], 16 * b + 16)
                pool.tensor_tensor(x1[:, :, :], x1[:, :, :], mod[:, 1:2, :].to_broadcast([P, NT, D]), ALU.add) \
                    .then_inc(S["xres_ready"], 1)

            def lo_of_h(s):
                for cc in range(KC):
                    wait_apart(pool, S["misc_drained"], use(s, f"F.hT{cc}") + 1)
                    pool.tensor_tensor(hT[:, 1, cc, :], tT[:, cc, :], hT[:, 0, cc, :], ALU.subtract) \
                        .then_inc(S["hT_lo"], 1)

            def inverse_rows(b):
                for hf in range(2):
                    inverse_std(1, 2 * hf, 2 * hf + 2, 2 * b + hf + 1)

            def finish_rows(b):
                for hf in range(2):
                    rows = on[:, 2 * hf:2 * hf + 2, :]
                    pool.wait_ge(S["z_ready"], 2 * b + hf + 1)
                    pool.tensor_tensor(rows, rows, mod[:, 2:3, :].to_broadcast([P, 2, D]), ALU.mult) \
                        .then_inc(S["zmul_ready"], 1)
                    pool.wait_ge(S["zmul_ready"], 2 * b + hf + 1)
                    pool.tensor_tensor(rows, rows, mod[:, 3:4, :].to_broadcast([P, 2, D]), ALU.add) \
                        .then_inc(S["h2_ready"], 1)
                for hf in range(2):
                    t = slice(2 * hf, 2 * hf + 2)
                    pool.wait_ge(S["hi_ready"], 2 * b + hf + 1)
                    pool.tensor_tensor(hl[:, t, D:2 * D], on[:, t, :], hl[:, t, 0:D], ALU.subtract) \
                        .then_inc(S["hl_ready"], 1)

            def scatter_rows(b):
                wait_apart(pool, S["rows_ready"], b + 1)
                wait_apart(pool, S["hl_ready"], 2 * b + 3)
                for t in range(NT):
                    for k in range(2):
                        pool.indirect_dma_start(
                            out=hx, out_offset=bass.IndirectOffsetOnAxis(ap=row_now[:, t, k:k + 1], axis=0),
                            in_=hl[:, t, :], in_offset=None).then_inc(S["scattered"], 16)
                wait_apart(pool, S["scattered"], 16 * 2 * NT * (b + 1))

            def step(g, par, back, front, *_):
                if front:
                    inverse_std(0, 0, NT, g + 2)
                if back:
                    residual_rows(g - 1)
                split_weights(g, 0)
                if back:
                    inverse_rows(g - 1)
                if front:
                    lo_of_h(g)
                if back:
                    finish_rows(g - 1)
                split_weights(g, 1)
                if back:
                    scatter_rows(g - 1)

            lo_of_h(-1)
            steps(pool, step)
            residual_rows(G - 1)
            inverse_rows(G - 1)
            finish_rows(G - 1)
            scatter_rows(G - 1)

            after_phase_a(pool)
            for n in range(2):
                pool.memset(small[:, 1:2], 0.0).then_inc(S["ysb_free"], 1)
                pool.wait_ge(S["ysb_free"], n + 1)

            def store_y(j, loc, par):
                pool.wait_ge(S["y_copied"], j + 1)
                pool.dma_start(yx[bass.ds(loc * GR, GR), :].rearrange("(t p) d -> p t d", p=P), ysb[:, par, :, :]) \
                    .then_inc(S["y_stored"], 16)
                wait_apart(pool, S["y_stored"], 16 * j + 16)
                pool.memset(small[:, 1:2], 0.0).then_inc(S["ysb_free"], 1)
                pool.wait_ge(S["ysb_free"], j + 3)

            def routed(j, j2, loc, par, first, last):
                if not first:
                    store_y(j - 1, loc - 1, 1 - par)
                if last:
                    store_y(j, loc, par)

            group_steps(pool, 0, NG1, routed)
            pool.wait_ge(S["y_stored"], 16 * NG1)
            pool.wait_ge(S["rows_moved"], 1)

            def fetch(loc, par):
                pool.tensor_copy(row_cur[:, par, :],
                                 row_all[:, bass.ds(loc * RT, RT), :].rearrange("p t k -> p (t k)")) \
                    .then_inc(S["rowcur_ready"], 1)
                pool.dma_start(x1b[:, par, :, :], x1d[bass.ds(loc * GR, GR), :]
                               .rearrange("(t p) d -> p t d", p=P)).then_inc(S["x1b_loaded"], 16)
                wait_apart(pool, S["rowcur_ready"], loc + 1)
                for t in range(RT):
                    for k in range(2):
                        pool.indirect_dma_start(
                            out=gy[:, par, t, k, :], out_offset=None, in_=yx,
                            in_offset=bass.IndirectOffsetOnAxis(ap=row_cur[:, par, 2 * t + k:2 * t + k + 1], axis=0)
                        ).then_inc(S["gathered"], 16)

            def shared(j, j2, loc, par, first, last):
                if not first:
                    pool.wait_ge(S["acc_ready"], loc)
                if not last:
                    pool.wait_ge(S["gathered"], 64 * (loc + 1))
                    pool.wait_ge(S["x1b_loaded"], 16 * (loc + 1))
                    fetch(loc + 1, 1 - par)

            fetch(0, 0)
            group_steps(pool, NG1, NG2, shared)

        @block.scalar
        def _(act):
            def load_x(f):
                act.dma_start(xin[:, :, :], x[bass.ds(f * GT, GT), :].rearrange("(t p) d -> p t d", p=P)) \
                    .then_inc(S["x_loaded"], 16)

            act.wait_ge(S["weights_in"], 16 * 9)
            for half, src in enumerate((pj, pj2)):
                act.activation(halves[half][:, 0:8 * FEAT], src, ACT.Copy).then_inc(S["proj_hi"], 1)
            for cc in range(KC):
                act.activation(wq_sb[:, 0, cc, :], wq_in[cc], ACT.Copy, scale=WSCALE).then_inc(S["wq_hi"], 1)
            act.wait_ge(S["proj_lo"], 1)
            load_x(0)
            act.wait_ge(S["cT_psum"], 1)
            act.activation(cT, misc[:, 0:KC * NBATCH].rearrange("p (c b) -> p c b", c=KC), ACT.Silu) \
                .then_inc(S["cT_ready"], 1)
            act.wait_ge(S["modT_psum"], 1)
            act.activation(modT[:, :, :, :].rearrange("p a b c -> p (a b c)"),
                           misc[:, 0:2 * KC * NBATCH], ACT.Copy).then_inc(S["modT_ready"], 1)
            act.wait_ge(S["modT_ready"], 1)
            act.wait_ge(S["wq_lo"], KC)

            def xn(f):
                act.wait_ge(S["rstd1_ready"], f + 1)
                for t in range(NT):
                    ins = act.activation(xin[:, t, :], xin[:, t, :], ACT.Identity,
                                         scale=rstd[:, 0, t, 0:1], bias=rstd[:, 0, t, 1:2])
                ins.then_inc(S["xn_ready"], 1)

            def read_scratch(s, what):
                wait_apart(act, S["misc_filled"], use(s, what) + 1)

            def front_piece(s, what, batch, vpar):
                read_scratch(s, what)
                if what[:4] == "F.hT":
                    cc = int(what[4])
                    for dst in (tT[:, cc, :], hT[:, 0, cc, :]):
                        ins = act.activation(dst, misc, ACT.Identity, scale=modT[:, 1, cc, bass.ds(batch, 1)],
                                             bias=modT[:, 0, cc, bass.ds(batch, 1)])
                    ins.then_inc(S["misc_drained"], 1)
                elif what[:3] == "F.v":
                    tp = int(what[3])
                    act.activation(v_sb[:, vpar, 2 * tp:2 * tp + 2, :, 0:DH].rearrange("p t h d -> p (t h) d"),
                                   misc.rearrange("p (t d) -> p t d", d=DH), ACT.Copy, scale=1.0 / WSCALE) \
                        .then_inc(S["misc_drained"], 1)
                else:
                    jj = ["F.q0", "F.k0", "F.q1", "F.k1"].index(what)
                    if not (isinstance(s, int) and s < 0):
                        act.wait_ge(stack_loaded[jj // 2], 16 * 12 * (s + 1))
                    act.activation(qk[:, jj, 0, :], misc, ACT.Copy, scale=1.0 / WSCALE).then_inc(S["qk_hi"], 1)

            def back_piece(s, what):
                if what[:4] in ("B.oT", "B.nT"):
                    read_scratch(s, what)
                    act.activation(tT[:, int(what[4]), :], misc, ACT.Copy).then_inc(S["misc_drained"], 1)
                elif what == "B.route":
                    read_scratch(s, what)
                    act.activation(gate[:, :, :].rearrange("p t e -> p (t e)"), misc[:, 0:NT * NE], ACT.Exp,
                                   scale=-1.0 / HSCALE).then_inc(S["misc_drained"], 1)

            def z(b, hf):
                act.wait_ge(S["rstd2_ready"], 2 * b + hf + 1)
                for t in (2 * hf, 2 * hf + 1):
                    ins = act.activation(on[:, t, :], x1[:, t, :], ACT.Identity,
                                         scale=rstd[:, 1, t, 0:1], bias=rstd[:, 1, t, 1:2])
                ins.then_inc(S["z_ready"], 1)

            def hi(b, hf):
                act.wait_ge(S["h2_ready"], 2 * b + hf + 1)
                act.activation(hl[:, 2 * hf:2 * hf + 2, 0:D], on[:, 2 * hf:2 * hf + 2, :], ACT.Copy) \
                    .then_inc(S["hi_ready"], 1)

            def exps(g, h):
                for k in range(2):
                    b = 2 * (h % 2) + k
                    act.wait_ge(S["feat_psum"], 32 * g + 2 * h + k + 1)
                    if k == 0 and not (isinstance(g, int) and g == 0 and h < 2):
                        act.wait_ge(S["scores_done"], 16 * g + h - 1)
                    act.activation(feat[:, b, :], ps[:, feat_bank(h, k), :], ACT.Exp, bias=small[:, 0:1]) \
                        .then_inc(S["exp_ready"], 1)

            def copy_o(g, pair):
                act.wait_ge(S["av_done"], 16 * g + 2 * pair + 2)
                lanes = [slice(0, 2)] if 2 * pair + 1 < H - AHEAD + 1 else [slice(0, 1), slice(1, 2)]
                for lane in lanes:
                    h = 2 * pair + lane.start
                    at = (h - first_of(h)) * VW
                    ins = act.activation(o_sb[:, 2 * pair + lane.start:2 * pair + lane.stop, :, :]
                                         .rearrange("p h t v -> p (h t) v"),
                                         ps[:, 5, :].rearrange("p (l t o) -> p l t o", l=2, o=OW)
                                         [:, lane, :, at:at + VW].rearrange("p l t v -> p (l t) v"), ACT.Copy)
                ins.then_inc(S["o_copied"], 1)

            def weights(g, r):
                act.wait_ge(S["w_loaded"], 32 * g + 16 * r + 16)
                act.activation(wst[:, :], wst[:, :], ACT.Copy, scale=WSCALE).then_inc(S["w_scaled"], 1)
                act.wait_ge(S["w_scaled"], 2 * g + r + 1)
                act.activation(whi[:, bass.ds(g * (2 * WPIECE) + r * WPIECE, WPIECE)], wst[:, :], ACT.Copy) \
                    .then_inc(S["w_hi"], 1)

            def step(g, par, back, front, batch_b, batch_f):
                if front:
                    load_x(g + 1)
                for h in range(H):
                    if h < H - 1:
                        exps(g, h + 1)
                    elif front:
                        exps(g + 1, 0)
                    if h == 1:
                        weights(g, 0)
                    if front and h == 4:
                        xn(g + 1)
                    if h == 14:
                        weights(g, 1)
                    if back and h in (7, 8):
                        z(g - 1, h - 7)
                    if back and h in (9, 10):
                        hi(g - 1, h - 9)
                    for half in (0, 0.5):
                        for what, at in PLAN:
                            if at == h + half and what[0] == "F" and front:
                                front_piece(g, what, batch_f, 1 - par)
                            if at == h + half and what[0] == "B" and back:
                                back_piece(g, what)
                        if half == 0 and h % 2 == 0:
                            if h:
                                copy_o(g, h // 2 - 1)
                            elif back:
                                copy_o(g - 1, PAIRS - 1)

            xn(0)
            for what in FRONT:
                front_piece(-1, what, 0, 0)
            act.wait_ge(S["prep_stored"], 14 * 16)
            exps(0, 0)
            steps(act, step)
            copy_o(G - 1, PAIRS - 1)
            for what in ("B.oT0", "B.oT1"):
                back_piece(G, what)
            z(G - 1, 0)
            z(G - 1, 1)
            hi(G - 1, 0)
            hi(G - 1, 1)
            for what in ("B.nT0", "B.nT1", "B.route"):
                back_piece(G, what)

            after_phase_a(act)

            def hidden(j, par):
                for hf in range(2):
                    act.wait_ge(S["ab_filled"], 2 * j + hf + 1)
                    act.activation(sil[:, hf, :, :], ps[:, 2 * hf, :].rearrange("p (c n) -> p c n", n=GR),
                                   ACT.Silu, scale=1.0 / (WSCALE * HSCALE)).then_inc(S["silu_ready"], 1)
                for hf in range(2):
                    act.wait_ge(S["g_ready"], 2 * j + hf + 1)
                    act.activation(ghi[:, par, 2 * hf:2 * hf + 2, :], g32[:, par, hf, :, :], ACT.Copy) \
                        .then_inc(S["ghi_ready"], 1)

            def copy_y(j, par):
                act.wait_ge(S["y_filled"], j + 1)
                act.wait_ge(S["ysb_free"], j + 1)
                act.activation(ysb[:, par, :, :], ps[:, 4 + par, :].rearrange("p (t d) -> p t d", d=D),
                               ACT.Copy).then_inc(S["y_copied"], 1)

            def routed(j, j2, loc, par, first, last):
                hidden(j, par)
                if not first:
                    copy_y(j - 1, 1 - par)

            def store_out(loc, par):
                act.wait_ge(S["acc_ready"], loc + 1)
                act.dma_start(out[bass.ds(loc * GR, GR), :].rearrange("(t p) d -> p t d", p=P), acc[:, par, :, :]) \
                    .then_inc(out_stored[par], 16)

            def shared(j, j2, loc, par, first, last):
                hidden(j, par)
                if first:
                    copy_y(j - 1, 1 - par)
                else:
                    store_out(loc - 1, 1 - par)
                if last:
                    store_out(loc, par)

            group_steps(act, 0, NG1, routed)
            for par in range(2):
                act.activation(small[:, 6 + par:7 + par], small[:, 0:1], ACT.Copy).then_inc(out_stored[par], 16)
            group_steps(act, NG1, NG2, shared)
            for par in range(2):
                act.wait_ge(out_stored[par], 16 + 16 * NG2 // 2)

        @block.vector
        def _(dve):
            def chain(name, start=0):
                count = [start]

                def link(ins):
                    count[0] = count[0] + 1
                    ins.then_inc(S[name], 1)
                    wait_apart(dve, S[name], count[0])
                return link

            dve.wait_ge(S["weights_in"], 16 * 9)
            for half, src in enumerate((pj, pj2)):
                dve.wait_ge(S["proj_hi"], half + 1)
                dve.tensor_tensor(halves[half][:, 8 * FEAT:16 * FEAT], src, halves[half][:, 0:8 * FEAT],
                                  ALU.subtract).then_inc(S["proj_lo"], 1)
            def stats(src, which, tiles, link):
                t0, t1 = tiles[0], tiles[-1] + 1
                for t in tiles:
                    ins = dve.bn_stats(st6[:, which, t, :], src[:, t, :])
                link(ins)
                for t in tiles:
                    ins = dve.bn_aggr(mv[:, which, t, :], st6[:, which, t, :])
                link(ins)
                dve.tensor_scalar(vn[:, which, t0:t1, 0], mv[:, which, t0:t1, 1], EPS_LN, None, ALU.add)
                ins = dve.tensor_scalar(vn[:, which, t0:t1, 1], mv[:, which, t0:t1, 0], -1.0, None, ALU.mult)
                ins.then_inc(S[("moments1", "moments2")[which]], 1)

            def front_stats(f):
                dve.wait_ge(S["x_loaded"], 16 * f + 16)
                if not (isinstance(f, int) and f == 0):
                    dve.wait_ge(S["xn_ready"], f)
                stats(xin, 0, range(NT), chain("stats_chain", 2 * f))

            for cc in range(KC):
                dve.wait_ge(S["wq_hi"], cc + 1)
                dve.scalar_tensor_tensor(wq_sb[:, 1, cc, :], wq_in[cc], WSCALE, wq_sb[:, 0, cc, :],
                                         ALU.mult, ALU.subtract).then_inc(S["wq_lo"], 1)
            front_stats(0)
            dve.wait_ge(S["mod_psum"], 1)
            mp = ps[0:NBATCH, 0:3, :].rearrange("p a (b n) -> p (a b) n", n=D)
            link = chain("mod_chain")
            link(dve.tensor_copy(m8[:, 0, :], mp[:, 0, :]))
            link(dve.tensor_scalar(m8[:, 1, :], mp[:, 1, :], 1.0, None, ALU.add))
            link(dve.tensor_scalar(rows8[:, 2, :], mp[:, 4, :], 1.0, HSCALE, ALU.add, ALU.mult))
            link(dve.tensor_scalar(rows8[:, 3, :], mp[:, 3, :], HSCALE, None, ALU.mult))
            for n, dst in ((2, rows8[:, 0, :]), (5, gb8)):
                link(dve.tensor_scalar(m8[:, 2, :], mp[:, n, :], 0.0, 2.0, ALU.is_ge, ALU.mult))
                link(dve.tensor_scalar(m8[:, 2, :], m8[:, 2, :], 1.0, None, ALU.subtract))
                link(dve.tensor_scalar(m8[:, 3, :], mp[:, n, :], -1.0, None, ALU.mult))
                link(dve.tensor_tensor(m8[:, 3, :], m8[:, 3, :], mp[:, n, :], ALU.max))
                link(dve.tensor_scalar(m8[:, 3, :], m8[:, 3, :], 0.25, None, ALU.max))
                link(dve.tensor_tensor(dst, m8[:, 2, :], m8[:, 3, :], ALU.mult))
            link(dve.tensor_tensor(rows8[:, 1, :], rows8[:, 0, :], bout8, ALU.mult))
            dve.tensor_scalar(gb8, gb8, 1.0 / (3.0 * GSCALE * WSCALE), None, ALU.mult) \
                .then_inc(S["mod_rows"], 1)

            def lo(s, what):
                jj = ["F.q0", "F.k0", "F.q1", "F.k1"].index(what)
                dve.wait_ge(S["qk_hi"], 4 * (s + 1) + jj + 1)
                dve.scalar_tensor_tensor(qk[:, jj, 1, :], misc, 1.0 / WSCALE, qk[:, jj, 0, :], ALU.mult, ALU.subtract) \
                    .then_inc(S["misc_drained"], 1)

            def features(g, h, k):
                b = 2 * (h % 2) + k
                dve.wait_ge(S["exp_ready"], 32 * g + 2 * h + k + 1)
                dve.scalar_tensor_tensor(feat[:, b, :], feat[:, b, :], 1.0, ps[:, feat_bank(h, k), :], ALU.min, ALU.max) \
                    .then_inc(S["feat_ready"], 1)

            def mask_scores(g, h):
                dve.wait_ge(S["scores_done"], 16 * g + h + 1)
                if not (isinstance(g, int) and g == 0 and h < 2):
                    dve.wait_ge(S["av_done"], 16 * g + h - 1)
                dve.tensor_tensor(att[:, h % 2, :].rearrange("p (t q) -> p t q", t=NT),
                                  ps[:, 3 + h % 2, :].rearrange("p (t q) -> p t q", t=NT),
                                  mask[:, :].unsqueeze(1).to_broadcast([P, NT, P]), ALU.mult) \
                    .then_inc(S["att_ready"], 1)

            def normalise(b):
                dve.wait_ge(S["o_copied"], PAIRS * b + PAIRS)
                wait_apart(dve, S["hl_ready"], 2 * b + 1)
                link = chain("den_chain", 2 * b)
                den = rden[:, :].rearrange("p (h t) -> p h t", t=NT)
                link(dve.tensor_scalar(den, o_sb[:, :, :, DH], EPS_Z, None, ALU.add))
                link(dve.reciprocal(rden[:, :], rden[:, :]))
                for t in range(NT):
                    ins = dve.tensor_tensor(on[:, t, :].rearrange("p (h d) -> p h d", d=DH), o_sb[:, :, t, 0:DH],
                                            den[:, :, t].unsqueeze(2).to_broadcast([P, H, DH]), ALU.mult)
                ins.then_inc(S["on_ready"], 1)

            def residual(b, s, hf):
                dve.wait_ge(S["misc_filled"], use(s, f"B.wo{hf}") + 1)
                dve.wait_ge(S["xres_ready"], b + 1)
                xg = on[:, 2 * hf:2 * hf + 2, :]
                dve.tensor_tensor(xg, misc.rearrange("p (t d) -> p t d", d=D),
                                  mod[:, 0:1, :].to_broadcast([P, 2, D]), ALU.mult).then_inc(S["misc_drained"], 1)
                dve.wait_ge(S["misc_drained"], use(s, f"B.wo{hf}") + 1)
                rows = x1[:, 2 * hf:2 * hf + 2, :]
                dve.tensor_tensor(rows, rows, xg, ALU.add).then_inc(S["x1_ready"], 1)

            def stats2(b, hf):
                dve.wait_ge(S["x1_ready"], 2 * b + hf + 1)
                stats(x1, 1, range(2 * hf, 2 * hf + 2), chain("stats2_chain", 4 * b + 2 * hf))

            def route(b, s, part):
                if part == 0:
                    dve.wait_ge(S["misc_drained"], use(s, "B.route") + 1)
                else:
                    wait_apart(dve, S["route_chain"], ROUTE * b + 2 * part)
                link = chain("route_chain", ROUTE * b + 2 * part)
                signal = lambda ins: ins.then_inc(S["route_chain"], 1)
                three = lambda v: v.unsqueeze(2).to_broadcast([P, NT, NE])
                revb = rev[:, :].unsqueeze(1).to_broadcast([P, NT, NE])
                gates, k, step_of_k = gate[:, :, :], int(part >= 4), (part - 1) % 3
                if part == 0:
                    link(dve.tensor_scalar(gates, gates, 1.0, None, ALU.add))
                    signal(dve.reciprocal(gates, gates))
                elif part < 7 and step_of_k == 0:
                    link(dve.tensor_reduce(top[:, k, :], gates, AX, ALU.max))
                    signal(dve.tensor_tensor(cmp_[:, :, :], gates, three(top[:, k, :]), ALU.is_equal))
                elif part < 7 and step_of_k == 1:
                    link(dve.tensor_tensor(cmp_[:, :, :], cmp_[:, :, :], revb, ALU.mult))
                    signal(dve.tensor_reduce(key[:, k, :], cmp_[:, :, :], AX, ALU.max))
                elif part < 7:
                    link(dve.tensor_tensor(oh[:, k, :, :], revb, three(key[:, k, :]), ALU.is_equal))
                    if k == 0:
                        signal(dve.scalar_tensor_tensor(gates, oh[:, 0, :, :], -2.0, gates, ALU.mult, ALU.add))
                    else:
                        signal(dve.tensor_tensor(ohs[:, :, :], oh[:, 0, :, :], oh[:, 1, :, :], ALU.add))
                elif part == 7:
                    link(dve.tensor_tensor(wsum[:, :], top[:, 0, :], top[:, 1, :], ALU.add))
                    signal(dve.reciprocal(wsum[:, :], wsum[:, :]))
                else:
                    for k in range(2):
                        signal(dve.tensor_tensor(gate_w[:, bass.ds(b * NT, NT), k], top[:, k, :], wsum[:, :],
                                                 ALU.mult))

            def rank(b, s, par):
                dve.wait_ge(S["misc_filled"], use(s, "B.rank") + 1)
                link = chain("rank_chain", 5 * b)
                dve.tensor_tensor(pos[:, par, :, :], misc[:, 0:(NT + 1) * NE].rearrange("p (t e) -> p t e", e=NE),
                                  pos[:, 1 - par, NT:NT + 1, :].to_broadcast([P, NT + 1, NE]), ALU.add) \
                    .then_inc(S["misc_drained"], 1)
                dve.wait_ge(S["misc_drained"], use(s, "B.rank") + 1)
                for k in range(2):
                    link(dve.tensor_tensor(oh[:, k, :, :], oh[:, k, :, :], pos[:, par, 0:NT, :], ALU.mult))
                    link(dve.tensor_reduce(rowf[:, :, k], oh[:, k, :, :], AX, ALU.add))
                link(dve.tensor_copy(row_all[:, bass.ds(b * NT, NT), :], rowf[:, :, :]))
                dve.tensor_copy(row_now[:, :, :], rowf[:, :, :]).then_inc(S["rows_ready"], 1)

            def step(g, par, back, front, *_):
                for h in range(H):
                    for k in range(2):
                        if h < H - 1:
                            features(g, h + 1, k)
                        elif front:
                            features(g + 1, 0, k)
                        if back and h >= H - PARTS // 3:
                            route(g - 1, g, 3 * (h - H) + PARTS + k)
                    mask_scores(g, h)
                    if front and h == 2:
                        front_stats(g + 1)
                    for what, at in PLAN:
                        if front and at == h and what[:3] in ("F.q", "F.k"):
                            lo(g, what)
                    if back:
                        if h == 1:
                            normalise(g - 1)
                        if h in (4, 5):
                            residual(g - 1, g, h - 4)
                            stats2(g - 1, h - 4)
                        if h >= H - PARTS // 3:
                            route(g - 1, g, 3 * (h - H) + PARTS + 2)
                        if h == 15:
                            rank(g - 1, g, 1 - par)

            dve.wait_ge(S["modT_psum"], 1)
            for what in ("F.q0", "F.k0", "F.q1", "F.k1"):
                lo(-1, what)
            for k in range(2):
                features(0, 0, k)
            steps(dve, step)
            b = G - 1
            normalise(b)
            for hf in range(2):
                residual(b, G, hf)
                stats2(b, hf)
            for part in range(PARTS):
                route(b, G, part)
            rank(b, G, 1)

            link = chain("table_chain")
            fin = pos[:, 1, NT, :]
            cols = lambda n: tab[0:1, n * NG1:(n + 1) * NG1]
            jj, ex, first_, row, off, ok = (cols(n) for n in range(6))
            big = tab[:, 8 * NG1:8 * NG1 + 4 * NE]
            start, ng, cum = (big[:, n * NE:(n + 1) * NE] for n in range(3))
            shift = small[:, 8:8 + NE]
            cube = tab[0:1, 16 * NG1:16 * NG1 + NG1 * NE].rearrange("p (j e) -> p j e", e=NE)
            link(dve.tensor_copy(tab_z[0:1, :], fin[0:1, :]))
            dve.memset(small[0:1, 2:3], 0.0).then_inc(S["rests_ready"], 1)
            link(dve.tensor_copy(jj, tab_r[0:1, :]))
            link(dve.tensor_scalar(start, rev[:, :], -float(REGION), float(REGION * NE), ALU.mult, ALU.add))
            link(dve.scalar_tensor_tensor(ng, fin, float(GR - 1), start, ALU.add, ALU.subtract))
            link(dve.tensor_copy(cnt_i[:, 0, :], ng))
            link(dve.tensor_scalar(cnt_i[:, 1, :], cnt_i[:, 0, :], GR.bit_length() - 1, None,
                                   ALU.arith_shift_right))
            link(dve.tensor_copy(ng, cnt_i[:, 1, :]))
            link(dve.tensor_scalar(shift, ng, float(GR), float(REGION), ALU.mult, ALU.subtract))
            start, ng, cum = start[0:1, :], ng[0:1, :], cum[0:1, :]
            link(dve.memset(start, 1.0))
            link(dve.tensor_tensor_scan(cum, start, ng, 0.0, ALU.mult, ALU.add))
            link(dve.tensor_tensor(cube, jj.unsqueeze(2).to_broadcast([1, NG1, NE]),
                                   cum.unsqueeze(1).to_broadcast([1, NG1, NE]), ALU.is_ge))
            link(dve.tensor_reduce(ex, cube, AX, ALU.add))
            link(dve.tensor_tensor(cube, cube, ng.unsqueeze(1).to_broadcast([1, NG1, NE]), ALU.mult))
            link(dve.tensor_reduce(first_, cube, AX, ALU.add))
            link(dve.tensor_scalar(ok, ex, NE - 0.5, None, ALU.is_le))
            link(dve.tensor_tensor(off, jj, first_, ALU.subtract))
            link(dve.tensor_scalar(off, off, float(GR), None, ALU.mult))
            link(dve.scalar_tensor_tensor(row, ex, float(REGION), off, ALU.mult, ALU.add))
            link(dve.tensor_scalar(off, row, float(DUMP), None, ALU.subtract))
            link(dve.tensor_tensor(off, off, ok, ALU.mult))
            link(dve.tensor_scalar(off, off, float(DUMP), None, ALU.add))
            link(dve.tensor_copy(tab_r[0:1, :], off))
            link(dve.tensor_scalar(ex, ex, float(NE - 1), None, ALU.min))
            link(dve.tensor_scalar(ex, ex, 1.0, float(EW), ALU.add, ALU.mult))
            dve.tensor_copy(tab_e[0:1, :], ex).then_inc(S["table_ready"], 1)
            after_phase_a(dve)

            def copy_hT(j, par):
                dve.wait_ge(S["tr_filled"], j + 1)
                dve.tensor_copy(hTr[:, par, :, :].rearrange("p c n -> p (c n)"), ps[:, 6, :].bitcast(F16)) \
                    .then_inc(S["hT_ready"], 1)

            def hidden(j, par, first, last):
                if not last:
                    copy_hT(j + 1, 1 - par)
                for hf in range(2):
                    dve.wait_ge(S["silu_ready"], 2 * j + hf + 1)
                    dve.scalar_tensor_tensor(g32[:, par, hf, :, :].rearrange("p c n -> p (c n)"), ps[:, 2 * hf + 1, :],
                                             GSCALE / (WSCALE * HSCALE),
                                             sil[:, hf, :, :].rearrange("p c n -> p (c n)"), ALU.mult, ALU.mult) \
                        .then_inc(S["g_ready"], 1)
                for hf in range(2):
                    dve.wait_ge(S["ghi_ready"], 2 * j + hf + 1)
                    dve.tensor_tensor(glo[:, par, 2 * hf:2 * hf + 2, :], g32[:, par, hf, :, :],
                                      ghi[:, par, 2 * hf:2 * hf + 2, :], ALU.subtract).then_inc(S["glo_ready"], 1)

            def routed(j, j2, loc, par, first, last):
                hidden(j, par, first, False)

            def combine(j, loc, par, batch):
                dve.wait_ge(S["y_filled"], j + 1)
                dve.wait_ge(S["gathered"], 64 * loc + 64)
                dve.wait_ge(S["x1b_loaded"], 16 * loc + 16)
                dve.wait_ge(out_stored[par], (loc - par) * 8 + 16)
                link = chain("comb_chain", 3 * loc)
                w = lambda t, k: gate_w[:, bass.ds(loc * RT + t, 1), k]
                for t in range(RT):
                    ins = dve.scalar_tensor_tensor(acc[:, par, t, :], gy[:, par, t, 0, :], w(t, 0),
                                                   ps[:, 4 + par, t * D:(t + 1) * D], ALU.mult, ALU.add)
                link(ins)
                for t in range(RT):
                    ins = dve.scalar_tensor_tensor(acc[:, par, t, :], gy[:, par, t, 1, :], w(t, 1),
                                                   acc[:, par, t, :], ALU.mult, ALU.add)
                link(ins)
                link(dve.tensor_tensor(acc[:, par, :, :], acc[:, par, :, :],
                                       gb_sb[:, bass.ds(batch, 1), :].to_broadcast([P, RT, D]), ALU.mult))
                dve.tensor_tensor(acc[:, par, :, :], acc[:, par, :, :], x1b[:, par, :, :], ALU.add) \
                    .then_inc(S["acc_ready"], 1)

            PB = T // NBATCH // GR

            def shared(j, j2, loc, par, first, last):
                hidden(j, par, first, last)
                if not first:
                    combine(j - 1, loc - 1, 1 - par, (loc - 1) // PB)
                if last:
                    combine(j, loc, par, loc // PB)

            copy_hT(0, 0)
            link = chain("row_chain")
            rows_i = row_all[:, :, :].rearrange("p t k -> p (t k)")
            link(dve.tensor_copy(rows_f[:, 0, :], rows_i))
            for e in range(1, NE):
                link(dve.tensor_scalar(rows_f[:, 1, :], rows_i, float(e * REGION), None, ALU.is_ge))
                link(dve.scalar_tensor_tensor(rows_f[:, 0, :], rows_f[:, 1, :], shift[:, e - 1:e], rows_f[:, 0, :],
                                              ALU.mult, ALU.add))
            dve.tensor_copy(rows_i, rows_f[:, 0, :]).then_inc(S["rows_moved"], 1)
            group_steps(dve, 0, NG1, routed)
            dve.wait_ge(S["gb_loaded"], 16)
            group_steps(dve, NG1, NG2, shared)

        @block.tensor
        def _(pe):
            pe.wait_ge(S["consts_ready"], 4)
            pe.wait_ge(S["weights_in"], 16 * 9)
            for cc in range(KC):
                ins = pe.transpose(misc[:, cc * NBATCH:(cc + 1) * NBATCH], c_sb[:, cc * P:(cc + 1) * P],
                                   ident[0:NBATCH, 0:NBATCH])
            ins.then_inc(S["cT_psum"], 1)
            pe.wait_ge(S["cT_ready"], 1)
            for n in range(3):
                for cc in range(KC):
                    ins = pe.matmul(ps[0:NBATCH, n, :], cT[:, cc, :], wmod_sb[:, cc, n * 512:(n + 1) * 512],
                                    start=(cc == 0), stop=(cc == KC - 1))
            ins.then_inc(S["mod_psum"], 1)
            pe.wait_ge(S["mod_chain"], 2)
            for r in range(2):
                for cc in range(KC):
                    at = (r * KC + cc) * NBATCH
                    ins = pe.transpose(misc[:, at:at + NBATCH], m8[:, r, cc * P:(cc + 1) * P],
                                       ident[0:NBATCH, 0:NBATCH])
            ins.then_inc(S["modT_psum"], 1)
            pe.wait_ge(S["modT_ready"], 1)

            def products(dst, pairs):
                for n, (w, h) in enumerate(pairs):
                    ins = pe.matmul(dst, w, h, start=(n == 0), stop=(n == len(pairs) - 1))
                return ins

            def scratch(s, what):
                u = use(s, what)
                if not (isinstance(u, int) and u == 0):
                    pe.wait_ge(S["misc_drained"], u)

            def front_piece(s, what, vpar):
                scratch(s, what)
                if what[:4] == "F.hT":
                    cc = int(what[4])
                    pe.wait_ge(S["xn_ready"], s + 2)
                    for t in range(NT):
                        ins = pe.transpose(misc[:, t * P:(t + 1) * P], xin[:, t, cc * P:(cc + 1) * P], ident[:, :])
                elif what[:3] == "F.v":
                    for t in range(2):
                        tok = (2 * int(what[3]) + t) * P
                        ins = products(misc[:, t * D:(t + 1) * D],
                                       [(hT[:, a, cc, tok:tok + P], wq_sb[:, b, cc, 2 * D:3 * D])
                                        for cc in range(KC) for a, b in ((0, 0), (0, 1), (1, 0))])
                else:
                    at = (0 if what[2] == "q" else D) + int(what[3]) * P
                    if what == "F.q0":
                        pe.wait_ge(S["hT_lo"], 2 * s + 4)
                    ins = products(misc, [(wq_sb[:, a, cc, at:at + P], hT[:, b, cc, :])
                                          for cc in range(KC) for a, b in ((0, 0), (0, 1), (1, 0))])
                ins.then_inc(S["misc_filled"], 1)

            def back_piece(s, b, what):
                scratch(s, what)
                if what[:4] in ("B.oT", "B.nT"):
                    cc = int(what[4])
                    if what[2] == "o":
                        pe.wait_ge(S["on_ready"], b + 1)
                    else:
                        pe.wait_ge(S["h2_ready"], 2 * b + 2)
                    for t in range(NT):
                        ins = pe.transpose(misc[:, t * P:(t + 1) * P], on[:, t, cc * P:(cc + 1) * P], ident[:, :])
                elif what[:4] == "B.wo":
                    for t in range(2):
                        for cc in range(KC):
                            tok = (2 * int(what[4]) + t) * P
                            ins = pe.matmul(misc[:, t * D:(t + 1) * D], tT[:, cc, tok:tok + P], wo_sb[:, cc, :],
                                            start=(cc == 0), stop=(cc == KC - 1))
                elif what == "B.route":
                    for t in range(NT):
                        for cc in range(KC):
                            ins = pe.matmul(misc[:, t * NE:(t + 1) * NE], tT[:, cc, t * P:(t + 1) * P],
                                            wg_sb[:, cc, :], start=(cc == 0), stop=(cc == KC - 1))
                else:
                    pe.wait_ge(S["route_chain"], ROUTE * b + ONEHOT)
                    for t in range(NT):
                        pe.matmul(misc[:, (t + 1) * NE:(NT + 1) * NE].rearrange("p (t e) -> p t e", e=NE),
                                  ones16[:, :], ohs[:, t:t + 1, :].to_broadcast([P, NT - t, NE]),
                                  start=(t == 0), stop=(t == NT - 1), skip_group_check=True)
                    ins = pe.matmul(misc[:, 0:NT * NE], tri[:, :], ohs[:, :, :].rearrange("p t e -> p (t e)"),
                                    start=False, stop=True, skip_group_check=True)
                ins.then_inc(S["misc_filled"], 1)

            def features(g, h):
                if h == 0:
                    pe.wait_ge(S["stack0_loaded"], 192 * g + 192)
                if h == 8:
                    pe.wait_ge(S["stack1_loaded"], 192 * g + 192)
                for k in range(2):
                    if k == 0 and not (isinstance(g, int) and g == 0 and h < 2):
                        pe.wait_ge(S["feat_ready"], 32 * g + 2 * h - 2)
                    if k == 1 and not (isinstance(g, int) and g == 0 and h < 2):
                        pe.wait_ge(S["feat_ready"], 32 * g + 2 * h - 1)
                    pe.matmul(ps[:, feat_bank(h, k), :], pst[:, h, :], stk[:, k, h // 2, :],
                              start=True, stop=True).then_inc(S["feat_psum"], 1)

            def scores(g, h):
                pe.wait_ge(S["feat_ready"], 32 * g + 2 * h + 2)
                if not (isinstance(g, int) and g == 0 and h < 2):
                    pe.wait_ge(S["att_ready"], 16 * g + h - 1)
                for t in range(NT):
                    tok = slice(t * P, (t + 1) * P)
                    ins = pe.matmul(ps[:, 3 + h % 2, tok], feat[:, 2 * (h % 2) + 1, tok],
                                    feat[:, 2 * (h % 2), tok], start=True, stop=True)
                ins.then_inc(S["scores_done"], 1)

            def weigh(g, h, par):
                pe.wait_ge(S["att_ready"], 16 * g + h + 1)
                pair = h // 2
                if h % 2 == 0 and not (isinstance(g, int) and g == 0 and pair < 1):
                    pe.wait_ge(S["o_copied"], PAIRS * g + pair)
                for t in range(NT):
                    at = ((h % 2) * NT + t) * OW
                    ins = pe.matmul(ps[:, 5, at:at + AHEAD * VW], att[:, h % 2, t * P:(t + 1) * P],
                                    v_sb[:, par, t, first_of(h):first_of(h) + AHEAD, :].rearrange("p h v -> p (h v)"),
                                    start=True, stop=True)
                ins.then_inc(S["av_done"], 1)

            def step(g, par, back, front, *_):
                for h in range(H):
                    if h < H - 1:
                        features(g, h + 1)
                    elif front:
                        features(g + 1, 0)
                    scores(g, h)
                    for half in (0, 0.5):
                        for what, at in PLAN:
                            if at == h + half and what[0] == "F" and front:
                                front_piece(g, what, 1 - par)
                            if at == h + half and what[0] == "B" and back:
                                back_piece(g, g - 1, what)
                        if half == 0:
                            if h:
                                weigh(g, h - 1, par)
                            elif back:
                                weigh(g - 1, H - 1, 1 - par)

            for what in FRONT:
                front_piece(-1, what, 0)
            pe.wait_ge(S["stk_ones"], 1)
            pe.wait_ge(S["misc_drained"], len(FRONT))
            features(0, 0)
            steps(pe, step)
            weigh(G - 1, H - 1, 1)
            for what in BACK:
                back_piece(G, G - 1, what)

            after_phase_a(pe)

            def turn(j, j2, par):
                pe.wait_ge(hrow_loaded[par], 16 * j2 + 16)
                if not (isinstance(j, int) and j == 0):
                    pe.wait_ge(S["hT_ready"], j)
                bank = ps[:, 6, :].bitcast(F16)
                for c4 in range(2 * KC):
                    for t in range(RT):
                        at = c4 * GR + t * P
                        ins = pe.transpose(bank[:, at:at + P], hrow[:, par, t, c4 * P:(c4 + 1) * P], ident16[:, :])
                ins.then_inc(S["tr_filled"], 1)

            def up(j, par, col):
                pe.wait_ge(S["hT_ready"], j + 1)
                for hf in range(2):
                    if not (isinstance(j, int) and j == 0):
                        pe.wait_ge(S["g_ready"], 2 * j - 1 + hf)
                    for m in range(2):
                        for f in range(2):
                            def w(half, cc):
                                at = col + ((m * KC + cc) * FF + (2 * hf + f) * P)
                                return half[:, bass.ds(at, P)]
                            h = lambda lane, cc: hTr[:, par, lane * KC + cc, :]
                            ins = products(ps[:, 2 * hf + m, f * GR:(f + 1) * GR],
                                           [q for cc in range(KC) for q in
                                            ((w(whi, cc), h(0, cc)), (w(whi, cc), h(1, cc)), (w(wlo, cc), h(0, cc)))])
                    ins.then_inc(S["ab_filled"], 1)

            def down(j, par, col):
                pe.wait_ge(S["glo_ready"], 2 * j + 2)
                for t in range(RT):
                    g = lambda half, f: half[:, par, f, t * P:(t + 1) * P]
                    w = lambda half, f: half[:, bass.ds(col + (2 * KC * FF + f * D), D)]
                    ins = products(ps[:, 4 + par, t * D:(t + 1) * D],
                                   [q for f in range(FC) for q in
                                    ((g(ghi, f), w(whi, f)), (g(ghi, f), w(wlo, f)), (g(glo, f), w(whi, f)))])
                ins.then_inc(S["y_filled"], 1)

            def column(loc):
                return pe.value_load(tab_e[0:1, bass.ds(loc, 1)], min_val=EW, max_val=NE * EW)

            def routed(j, j2, loc, par, first, last):
                turn(j + 1, j2 + par, 1 - par)
                up(j, par, column(loc))
                if not first:
                    down(j - 1, 1 - par, column(loc - 1))

            def shared(j, j2, loc, par, first, last):
                if not last:
                    turn(j + 1, j2 + par, 1 - par)
                up(j, par, 0)
                down(j - 1, 1 - par, column(NG1 - 1) if first else 0)
                if last:
                    down(j, par, 0)

            turn(0, 0, 0)
            group_steps(pe, 0, NG1, routed)
            group_steps(pe, NG1, NG2, shared)


def _by_partition(w, chunk=128):
    n = w.shape[0] // chunk
    return w.reshape(n, chunk, w.shape[1]).transpose(1, 0, 2).reshape(chunk, -1)


def kernel(**inputs):
    import numpy as np
    import concourse.bacc as bacc
    from concourse.bass_utils import run_bass_kernel_spmd

    a = {k: np.asarray(v) for k, v in inputs.items()}
    experts = [(a["L0_ffn_Ws1"], a["L0_ffn_Ws3"], a["L0_ffn_Ws2"])]
    experts += [(a["L0_ffn_We1"][e], a["L0_ffn_We3"][e], a["L0_ffn_We2"][e])
                for e in range(a["L0_ffn_We1"].shape[0])]
    x = a["L0_attn_x"]
    arrays = {
        "x": x.reshape(-1, x.shape[-1]), "wqkv": a["L0_attn_Wqkv"], "proj": a["L0_attn_proj"],
        "wout": a["L0_attn_Wout"], "bout": a["L0_attn_bout"], "wg": a["L0_ffn_Wg"],
        "wexp": np.concatenate([_by_partition(w) for e in experts for w in e], axis=1),
        "c": a["L0_c"], "wmod": a["L0_wmod"],
    }
    arrays = {k: np.ascontiguousarray(v) for k, v in arrays.items()}
    nc = bacc.Bacc("TRN2", target_bir_lowering=False, num_devices=1)
    args = {k: nc.dram_tensor(f"in_{k}", v.shape, mybir.dt.from_np(v.dtype), kind="ExternalInput").ap()
            for k, v in arrays.items()}
    out = nc.dram_tensor("out", arrays["x"].shape, F32, kind="ExternalOutput").ap()
    adaln_kernel(nc, out=out, **args)
    r = run_bass_kernel_spmd(nc, [{f"in_{k}": v for k, v in arrays.items()}], core_ids=[0])
    return r.results[0]["out"].reshape(x.shape)
```
